# Optimizing a Trainium2 kernel written in Bass

```python
import numpy as np
import jax
import jax.numpy as jnp

def _softmax(x, axis=-1):
    return jax.nn.softmax(x, axis=axis)

def _gelu(x):
    return jax.nn.gelu(x, approximate=True)

def _silu(x):
    return jax.nn.silu(x)

def _sigmoid(x):
    return jax.nn.sigmoid(x)

def _layernorm(x, axis=-1, eps=1e-05):
    m = jnp.mean(x, axis=axis, keepdims=True)
    v = jnp.var(x, axis=axis, keepdims=True)
    return (x - m) / jnp.sqrt(v + eps)

def _scatter_add(tgt, idx, src, axis=0):
    return tgt.at[idx].add(src)

def _segment_sum(src, seg, n):
    return jax.ops.segment_sum(src, seg, n)
kernel_name = 'mk_decoder_preln_d2_seqx_r8_756289'

def setup_inputs(seed: int=0):
    np.random.seed(seed)
    _w = jnp.asarray

    def _rec_inputs():
        import jax
        import jax.numpy as jnp
        _rk = jax.random.key(seed)
        x = -0.0002928 + 1 * jax.random.normal(jax.random.fold_in(_rk, 1), (64, 64, 128), jnp.float32)
        _lenS = 64 - jax.random.randint(jax.random.fold_in(_rk, 7), (64,), 0, max(1, 64 // 4) + 1, jnp.int32)
        _lenS2 = 64 - jax.random.randint(jax.random.fold_in(_rk, 8), (64,), 0, max(1, 64 // 4) + 1, jnp.int32)
        _ctx_512P = jax.random.normal(jax.random.fold_in(_rk, 11), (64, 16, 64), jnp.float32)
        _ctx_512c = jax.random.dirichlet(jax.random.fold_in(_rk, 511), 0.3 * jnp.ones((16,), jnp.float32), (64, 64))
        _ctx_512t = jnp.einsum('bsk,bkd->bsd', _ctx_512c, _ctx_512P)
        _ctx_512t = _ctx_512t * jax.lax.rsqrt(jnp.mean(jnp.square(_ctx_512t)) + 1e-12) * 0.953939
        ctx_512 = 0.00222621 + 0.99962 * (_ctx_512t + 0.3 * jax.random.normal(jax.random.fold_in(_rk, 611), (64, 64, 64), jnp.float32))
        itok_BxS2xS_0_7 = jax.random.randint(jax.random.fold_in(_rk, 12), (64, 64, 64), 0, 8, jnp.int32)
        return (x, ctx_512, itok_BxS2xS_0_7)
    x, ctx_512, itok_BxS2xS_0_7 = _rec_inputs()

    def _L0_attn_setup():
        import jax, jax.numpy as jnp
        import numpy as np
        import math
        B, L, D_MODEL = (8, 256, 128)
        D_INNER, D_SSM = (256, 128)
        KEY_DIM, VALUE_DIM, H = (96, 192, 4)
        DK, DV = (KEY_DIM // H, VALUE_DIM // H)
        D_CONV = 4
        EPS = 1e-05

        def _dwconv(x, w, b):
            y = jax.lax.conv_general_dilated(x, w, window_strides=(1,), padding=[(1, 2)], dimension_numbers=('NCH', 'OIH', 'NCH'), feature_group_count=x.shape[1])
            return y + b[None, :, None]

        def _l2norm(x):
            return x * jax.lax.rsqrt(jnp.sum(x * x, axis=-1, keepdims=True) + 1e-06)

        def _gated_delta_rule(q, k, v, beta, gk):
            qT = jnp.moveaxis(q, 2, 0)
            kT = jnp.moveaxis(k, 2, 0)
            vT = jnp.moveaxis(v, 2, 0)
            bT = jnp.moveaxis(beta, 2, 0)
            gT = jnp.moveaxis(gk, 2, 0)
            S0 = jnp.zeros((q.shape[0], q.shape[1], q.shape[3], v.shape[3]), q.dtype)

            def step(S, inp):
                qt, kt, vt, bt, gt = inp
                S = S * jnp.exp(gt)[..., None, None]
                u = bt[..., None] * (vt - jnp.einsum('bhk,bhkv->bhv', kt, S))
                S = S + jnp.einsum('bhk,bhv->bhkv', kt, u)
                ot = jnp.einsum('bhk,bhkv->bhv', qt, S)
                return (S, ot)
            _, o = jax.lax.scan(step, S0, (qT, kT, vT, bT, gT))
            return jnp.moveaxis(o, 0, 2)
        key = jax.random.key(seed)
        ks = jax.random.split(key, 20)

        def w(k, shape, fan_in):
            return jax.random.normal(k, shape, jnp.float32) / np.sqrt(fan_in)
        dt = jnp.exp(jax.random.uniform(ks[14], (H,)) * (math.log(0.1) - math.log(0.001)) + math.log(0.001))
        dt = jnp.clip(dt, 0.0001)
        dt_bias = dt + jnp.log(-jnp.expm1(-dt))
        A = jax.random.uniform(ks[13], (H,), minval=0.5, maxval=16.0)
        return {'x': jax.random.normal(ks[0], (B, L, D_MODEL), jnp.float32), 'W_in': w(ks[1], (D_MODEL, D_INNER), D_MODEL), 'conv_x_w': w(ks[2], (D_SSM, 1, D_CONV), D_CONV), 'conv_x_b': jnp.zeros((D_SSM,), jnp.float32), 'conv_z_w': w(ks[3], (D_SSM, 1, D_CONV), D_CONV), 'conv_z_b': jnp.zeros((D_SSM,), jnp.float32), 'W_q': w(ks[4], (D_SSM, KEY_DIM), D_SSM), 'W_k': w(ks[5], (D_SSM, KEY_DIM), D_SSM), 'W_v': w(ks[6], (D_SSM, VALUE_DIM), D_SSM), 'W_g': w(ks[7], (D_SSM, VALUE_DIM), D_SSM), 'W_gk': w(ks[8], (D_SSM, H), D_SSM), 'W_b': w(ks[9], (D_SSM, H), D_SSM), 'b_b': jnp.zeros((H,), jnp.float32), 'A_log': jnp.log(A), 'dt_bias': dt_bias, 'g_norm_w': jnp.ones((DV,), jnp.float32), 'W_so': w(ks[10], (VALUE_DIM, D_SSM), VALUE_DIM), 'W_out': w(ks[11], (D_INNER, D_MODEL), D_INNER)}
    _L0_attn_all = _L0_attn_setup()
    _L0_attn_in = {k: v for k, v in _L0_attn_all.items() if k in ('W_in', 'conv_x_w', 'conv_x_b', 'conv_z_w', 'conv_z_b', 'W_q', 'W_k', 'W_v', 'W_g', 'W_gk', 'W_b', 'b_b', 'A_log', 'dt_bias', 'g_norm_w', 'W_so', 'W_out')}
    del _L0_attn_all

    def _L0_xattn_setup():
        import jax, jax.numpy as jnp
        import numpy as np
        H, D, C1, C2, S, M, B, W = (16, 32, 128, 64, 256, 64, 2, 4)

        def _ln(x, g, b):
            m = jnp.mean(x, -1, keepdims=True)
            v = jnp.var(x, -1, keepdims=True)
            return (x - m) * jax.lax.rsqrt(v + 1e-05) * g + b

        def _mha(x, y, wq, wk, wv, li1_w, li1_b, lnx_g, lnx_b, lny_g, lny_b, ln3_g, ln3_b, li2_w, li2_b, li3_w, li3_b, causal):
            xn = _ln(x, lnx_g, lnx_b)
            yn = _ln(y, lny_g, lny_b)
            q = jnp.einsum('bsc,hcd->bhsd', xn, wq)
            k = jnp.einsum('btc,hcd->bhtd', yn, wk)
            v = jnp.einsum('btc,hcd->bhtd', yn, wv)
            a = jax.nn.softmax(jnp.einsum('bhsd,bhtd->bhst', q, k) * D ** (-0.5), axis=-1)
            if causal:
                s, t = (a.shape[-2], a.shape[-1])
                mask = (jnp.arange(t)[None, :] > jnp.arange(s)[:, None]).astype(a.dtype)
                a = a * mask
            o = jnp.einsum('bhst,bhtd->bhsd', a, v)
            o = o.transpose(0, 2, 1, 3).reshape(x.shape[0], x.shape[1], H * D)
            x_out = x + o @ li1_w + li1_b
            h = jax.nn.gelu(_ln(x_out, ln3_g, ln3_b) @ li2_w + li2_b, approximate=False)
            return x_out + h @ li3_w + li3_b
        key = jax.random.key(seed)
        ks = iter(jax.random.split(key, 64))

        def w(shape, scale=0.02):
            return jax.random.normal(next(ks), shape, jnp.float32) * scale
        inp = {'xx': jax.random.normal(next(ks), (B, S, C1), jnp.float32), 'ee': jax.random.normal(next(ks), (B, M, C2), jnp.float32), 'ln1_g': jnp.ones(C1, jnp.float32), 'ln1_b': jnp.zeros(C1, jnp.float32), 'ln2_g': jnp.ones(C1, jnp.float32), 'ln2_b': jnp.zeros(C1, jnp.float32)}
        for pfx, cy in (('a1', C1), ('a2', C2)):
            inp[pfx + '_wq'] = w((H, C1, D))
            inp[pfx + '_wk'] = w((H, cy, D))
            inp[pfx + '_wv'] = w((H, cy, D))
            inp[pfx + '_li1_w'] = w((H * D, C1))
            inp[pfx + '_li1_b'] = jnp.zeros(C1, jnp.float32)
            inp[pfx + '_lnx_g'] = jnp.ones(C1, jnp.float32)
            inp[pfx + '_lnx_b'] = jnp.zeros(C1, jnp.float32)
            inp[pfx + '_lny_g'] = jnp.ones(cy, jnp.float32)
            inp[pfx + '_lny_b'] = jnp.zeros(cy, jnp.float32)
            inp[pfx + '_ln3_g'] = jnp.ones(C1, jnp.float32)
            inp[pfx + '_ln3_b'] = jnp.zeros(C1, jnp.float32)
            inp[pfx + '_li2_w'] = w((C1, C1 * W))
            inp[pfx + '_li2_b'] = jnp.zeros(C1 * W, jnp.float32)
            inp[pfx + '_li3_w'] = w((C1 * W, C1))
            inp[pfx + '_li3_b'] = jnp.zeros(C1, jnp.float32)
        inp['training'] = 0
        return inp
    _L0_xattn_all = _L0_xattn_setup()
    _L0_xattn_in = {k: v for k, v in _L0_xattn_all.items() if k in ('ln1_g', 'ln1_b', 'ln2_g', 'ln2_b', 'a1_wq', 'a1_wk', 'a1_wv', 'a1_li1_w', 'a1_li1_b', 'a1_lnx_g', 'a1_lnx_b', 'a1_lny_g', 'a1_lny_b', 'a1_ln3_g', 'a1_ln3_b', 'a1_li2_w', 'a1_li2_b', 'a1_li3_w', 'a1_li3_b', 'a2_wq', 'a2_wk', 'a2_wv', 'a2_li1_w', 'a2_li1_b', 'a2_lnx_g', 'a2_lnx_b', 'a2_lny_g', 'a2_lny_b', 'a2_ln3_g', 'a2_ln3_b', 'a2_li2_w', 'a2_li2_b', 'a2_li3_w', 'a2_li3_b')}
    del _L0_xattn_all

    def _L0_ffn_setup():
        import jax, jax.numpy as jnp
        import numpy as np
        S, B, D, H, E, K, F = (128, 4, 128, 16, 8, 2, 512)

        def _ln(x, g, b, eps=1e-05):
            mu = jnp.mean(x, axis=-1, keepdims=True)
            var = jnp.mean((x - mu) ** 2, axis=-1, keepdims=True)
            return (x - mu) * jax.lax.rsqrt(var + eps) * g + b
        key = jax.random.key(seed)
        ks = jax.random.split(key, 8)
        s = 0.02
        return {'src': jax.random.normal(ks[0], (S, B, D), jnp.float32), 'in_proj_w': jax.random.normal(ks[1], (3 * D, D), jnp.float32) * s, 'in_proj_b': jnp.zeros((3 * D,), jnp.float32), 'out_w': jax.random.normal(ks[2], (D, D), jnp.float32) * s, 'out_b': jnp.zeros((D,), jnp.float32), 'gate_w': jax.random.normal(ks[3], (E, D), jnp.float32) * s, 'gate_b': jnp.zeros((E,), jnp.float32), 'w1': jax.random.normal(ks[4], (E, F, D), jnp.float32) * s, 'b1': jnp.zeros((E, F), jnp.float32), 'w2': jax.random.normal(ks[5], (E, D, F), jnp.float32) * s, 'b2': jnp.zeros((E, D), jnp.float32), 'ln1_g': jnp.ones((D,), jnp.float32), 'ln1_b': jnp.zeros((D,), jnp.float32), 'ln2_g': jnp.ones((D,), jnp.float32), 'ln2_b': jnp.zeros((D,), jnp.float32)}
    _L0_ffn_all = _L0_ffn_setup()
    _L0_ffn_in = {k: v for k, v in _L0_ffn_all.items() if k in ('in_proj_w', 'in_proj_b', 'out_w', 'out_b', 'gate_w', 'gate_b', 'w1', 'b1', 'w2', 'b2', 'ln1_g', 'ln1_b', 'ln2_g', 'ln2_b')}
    del _L0_ffn_all

    def _L1_attn_setup():
        import jax, jax.numpy as jnp
        import numpy as np
        DIM = 128
        HEADS = 16
        SCALE = DIM ** (-0.5)
        key = jax.random.key(seed)
        k1, k2, k3, k4 = jax.random.split(key, 4)
        x = jax.random.normal(k1, (2, 256, DIM), dtype=jnp.float32)
        w_qkv = jax.random.normal(k2, (DIM, 3 * DIM), dtype=jnp.float32) * DIM ** (-0.5)
        w_out = jax.random.normal(k3, (DIM, DIM), dtype=jnp.float32) * DIM ** (-0.5)
        b_out = jax.random.normal(k4, (DIM,), dtype=jnp.float32) * 0.01
        return {'x': x, 'w_qkv': w_qkv, 'w_out': w_out, 'b_out': b_out}
    _L1_attn_all = _L1_attn_setup()
    _L1_attn_in = {k: v for k, v in _L1_attn_all.items() if k in ('w_qkv', 'w_out', 'b_out')}
    del _L1_attn_all

    def _L1_xattn_setup():
        import jax, jax.numpy as jnp
        import numpy as np
        key = jax.random.key(seed)
        k1, k2, k3, k4, k5 = jax.random.split(key, 5)
        B, K, S, E, I, D = (4, 2, 64, 8, 128, 256)
        x = jax.random.normal(k1, (B, S, I), dtype=jnp.float32)
        weights = jax.random.uniform(k2, (B, K, S), dtype=jnp.float32)
        ensembles = jax.random.randint(k3, (B, K, S), 0, E, dtype=jnp.int64)
        lim1 = float(np.sqrt(6.0 / (D + I)))
        proj_in = jax.random.uniform(k4, (E, D, I), dtype=jnp.float32, minval=-lim1, maxval=lim1)
        proj_out = jax.random.uniform(k5, (E, I, D), dtype=jnp.float32, minval=-lim1, maxval=lim1)
        return {'x': x, 'weights': weights, 'ensembles': ensembles, 'proj_in': proj_in, 'proj_out': proj_out}
    _L1_xattn_all = _L1_xattn_setup()
    _L1_xattn_in = {k: v for k, v in _L1_xattn_all.items() if k in ('proj_in', 'proj_out')}
    del _L1_xattn_all

    def _L1_ffn_setup():
        import jax, jax.numpy as jnp
        import numpy as np
        D_MODEL, D_FF, N_EXPERTS, TOP_K = (128, 512, 8, 2)
        key = jax.random.key(seed)
        k0, k1, k2, k3 = jax.random.split(key, 4)
        x = jax.random.normal(k0, (2, 256, D_MODEL), dtype=jnp.float32)
        Wg = jax.random.normal(k1, (D_MODEL, N_EXPERTS), dtype=jnp.float32) * 0.02
        W1 = jax.random.normal(k2, (N_EXPERTS, D_MODEL, D_FF), dtype=jnp.float32) * 0.02
        b1 = jnp.zeros((N_EXPERTS, D_FF), dtype=jnp.float32)
        W2 = jax.random.normal(k3, (N_EXPERTS, D_FF, D_MODEL), dtype=jnp.float32) * 0.02
        b2 = jnp.zeros((N_EXPERTS, D_MODEL), dtype=jnp.float32)
        return {'x': x, 'Wg': Wg, 'W1': W1, 'b1': b1, 'W2': W2, 'b2': b2}
    _L1_ffn_all = _L1_ffn_setup()
    _L1_ffn_in = {k: v for k, v in _L1_ffn_all.items() if k in ('Wg', 'W1', 'b1', 'W2', 'b2')}
    del _L1_ffn_all
    return {'x': x, 'ctx_512': ctx_512, 'itok_BxS2xS_0_7': itok_BxS2xS_0_7, 'L0_attn_W_in': _L0_attn_in['W_in'], 'L0_attn_conv_x_w': _L0_attn_in['conv_x_w'], 'L0_attn_conv_x_b': _L0_attn_in['conv_x_b'], 'L0_attn_conv_z_w': _L0_attn_in['conv_z_w'], 'L0_attn_conv_z_b': _L0_attn_in['conv_z_b'], 'L0_attn_W_q': _L0_attn_in['W_q'], 'L0_attn_W_k': _L0_attn_in['W_k'], 'L0_attn_W_v': _L0_attn_in['W_v'], 'L0_attn_W_g': _L0_attn_in['W_g'], 'L0_attn_W_gk': _L0_attn_in['W_gk'], 'L0_attn_W_b': _L0_attn_in['W_b'], 'L0_attn_b_b': _L0_attn_in['b_b'], 'L0_attn_A_log': _L0_attn_in['A_log'], 'L0_attn_dt_bias': _L0_attn_in['dt_bias'], 'L0_attn_g_norm_w': _L0_attn_in['g_norm_w'], 'L0_attn_W_so': _L0_attn_in['W_so'], 'L0_attn_W_out': _L0_attn_in['W_out'], 'L0_xattn_ln1_g': _L0_xattn_in['ln1_g'], 'L0_xattn_ln1_b': _L0_xattn_in['ln1_b'], 'L0_xattn_ln2_g': _L0_xattn_in['ln2_g'], 'L0_xattn_ln2_b': _L0_xattn_in['ln2_b'], 'L0_xattn_a1_wq': _L0_xattn_in['a1_wq'], 'L0_xattn_a1_wk': _L0_xattn_in['a1_wk'], 'L0_xattn_a1_wv': _L0_xattn_in['a1_wv'], 'L0_xattn_a1_li1_w': _L0_xattn_in['a1_li1_w'], 'L0_xattn_a1_li1_b': _L0_xattn_in['a1_li1_b'], 'L0_xattn_a1_lnx_g': _L0_xattn_in['a1_lnx_g'], 'L0_xattn_a1_lnx_b': _L0_xattn_in['a1_lnx_b'], 'L0_xattn_a1_lny_g': _L0_xattn_in['a1_lny_g'], 'L0_xattn_a1_lny_b': _L0_xattn_in['a1_lny_b'], 'L0_xattn_a1_ln3_g': _L0_xattn_in['a1_ln3_g'], 'L0_xattn_a1_ln3_b': _L0_xattn_in['a1_ln3_b'], 'L0_xattn_a1_li2_w': _L0_xattn_in['a1_li2_w'], 'L0_xattn_a1_li2_b': _L0_xattn_in['a1_li2_b'], 'L0_xattn_a1_li3_w': _L0_xattn_in['a1_li3_w'], 'L0_xattn_a1_li3_b': _L0_xattn_in['a1_li3_b'], 'L0_xattn_a2_wq': _L0_xattn_in['a2_wq'], 'L0_xattn_a2_wk': _L0_xattn_in['a2_wk'], 'L0_xattn_a2_wv': _L0_xattn_in['a2_wv'], 'L0_xattn_a2_li1_w': _L0_xattn_in['a2_li1_w'], 'L0_xattn_a2_li1_b': _L0_xattn_in['a2_li1_b'], 'L0_xattn_a2_lnx_g': _L0_xattn_in['a2_lnx_g'], 'L0_xattn_a2_lnx_b': _L0_xattn_in['a2_lnx_b'], 'L0_xattn_a2_lny_g': _L0_xattn_in['a2_lny_g'], 'L0_xattn_a2_lny_b': _L0_xattn_in['a2_lny_b'], 'L0_xattn_a2_ln3_g': _L0_xattn_in['a2_ln3_g'], 'L0_xattn_a2_ln3_b': _L0_xattn_in['a2_ln3_b'], 'L0_xattn_a2_li2_w': _L0_xattn_in['a2_li2_w'], 'L0_xattn_a2_li2_b': _L0_xattn_in['a2_li2_b'], 'L0_xattn_a2_li3_w': _L0_xattn_in['a2_li3_w'], 'L0_xattn_a2_li3_b': _L0_xattn_in['a2_li3_b'], 'L0_ffn_in_proj_w': _L0_ffn_in['in_proj_w'], 'L0_ffn_in_proj_b': _L0_ffn_in['in_proj_b'], 'L0_ffn_out_w': _L0_ffn_in['out_w'], 'L0_ffn_out_b': _L0_ffn_in['out_b'], 'L0_ffn_gate_w': _L0_ffn_in['gate_w'], 'L0_ffn_gate_b': _L0_ffn_in['gate_b'], 'L0_ffn_w1': _L0_ffn_in['w1'], 'L0_ffn_b1': _L0_ffn_in['b1'], 'L0_ffn_w2': _L0_ffn_in['w2'], 'L0_ffn_b2': _L0_ffn_in['b2'], 'L0_ffn_ln1_g': _L0_ffn_in['ln1_g'], 'L0_ffn_ln1_b': _L0_ffn_in['ln1_b'], 'L0_ffn_ln2_g': _L0_ffn_in['ln2_g'], 'L0_ffn_ln2_b': _L0_ffn_in['ln2_b'], 'L1_attn_w_qkv': _L1_attn_in['w_qkv'], 'L1_attn_w_out': _L1_attn_in['w_out'], 'L1_attn_b_out': _L1_attn_in['b_out'], 'L1_xattn_proj_in': _L1_xattn_in['proj_in'], 'L1_xattn_proj_out': _L1_xattn_in['proj_out'], 'L1_ffn_Wg': _L1_ffn_in['Wg'], 'L1_ffn_W1': _L1_ffn_in['W1'], 'L1_ffn_b1': _L1_ffn_in['b1'], 'L1_ffn_W2': _L1_ffn_in['W2'], 'L1_ffn_b2': _L1_ffn_in['b2']}

def reference(x, ctx_512, itok_BxS2xS_0_7, L0_attn_W_in, L0_attn_conv_x_w, L0_attn_conv_x_b, L0_attn_conv_z_w, L0_attn_conv_z_b, L0_attn_W_q, L0_attn_W_k, L0_attn_W_v, L0_attn_W_g, L0_attn_W_gk, L0_attn_W_b, L0_attn_b_b, L0_attn_A_log, L0_attn_dt_bias, L0_attn_g_norm_w, L0_attn_W_so, L0_attn_W_out, L0_xattn_ln1_g, L0_xattn_ln1_b, L0_xattn_ln2_g, L0_xattn_ln2_b, L0_xattn_a1_wq, L0_xattn_a1_wk, L0_xattn_a1_wv, L0_xattn_a1_li1_w, L0_xattn_a1_li1_b, L0_xattn_a1_lnx_g, L0_xattn_a1_lnx_b, L0_xattn_a1_lny_g, L0_xattn_a1_lny_b, L0_xattn_a1_ln3_g, L0_xattn_a1_ln3_b, L0_xattn_a1_li2_w, L0_xattn_a1_li2_b, L0_xattn_a1_li3_w, L0_xattn_a1_li3_b, L0_xattn_a2_wq, L0_xattn_a2_wk, L0_xattn_a2_wv, L0_xattn_a2_li1_w, L0_xattn_a2_li1_b, L0_xattn_a2_lnx_g, L0_xattn_a2_lnx_b, L0_xattn_a2_lny_g, L0_xattn_a2_lny_b, L0_xattn_a2_ln3_g, L0_xattn_a2_ln3_b, L0_xattn_a2_li2_w, L0_xattn_a2_li2_b, L0_xattn_a2_li3_w, L0_xattn_a2_li3_b, L0_ffn_in_proj_w, L0_ffn_in_proj_b, L0_ffn_out_w, L0_ffn_out_b, L0_ffn_gate_w, L0_ffn_gate_b, L0_ffn_w1, L0_ffn_b1, L0_ffn_w2, L0_ffn_b2, L0_ffn_ln1_g, L0_ffn_ln1_b, L0_ffn_ln2_g, L0_ffn_ln2_b, L1_attn_w_qkv, L1_attn_w_out, L1_attn_b_out, L1_xattn_proj_in, L1_xattn_proj_out, L1_ffn_Wg, L1_ffn_W1, L1_ffn_b1, L1_ffn_W2, L1_ffn_b2):
    import jax
    import jax.numpy as jnp

    def _L0_attn_ref(x, W_in, conv_x_w, conv_x_b, conv_z_w, conv_z_b, W_q, W_k, W_v, W_g, W_gk, W_b, b_b, A_log, dt_bias, g_norm_w, W_so, W_out):
        import jax, jax.numpy as jnp
        import numpy as np
        import math
        B, L, D_MODEL = (8, 256, 128)
        D_INNER, D_SSM = (256, 128)
        KEY_DIM, VALUE_DIM, H = (96, 192, 4)
        DK, DV = (KEY_DIM // H, VALUE_DIM // H)
        D_CONV = 4
        EPS = 1e-05

        def _dwconv(x, w, b):
            y = jax.lax.conv_general_dilated(x, w, window_strides=(1,), padding=[(1, 2)], dimension_numbers=('NCH', 'OIH', 'NCH'), feature_group_count=x.shape[1])
            return y + b[None, :, None]

        def _l2norm(x):
            return x * jax.lax.rsqrt(jnp.sum(x * x, axis=-1, keepdims=True) + 1e-06)

        def _gated_delta_rule(q, k, v, beta, gk):
            qT = jnp.moveaxis(q, 2, 0)
            kT = jnp.moveaxis(k, 2, 0)
            vT = jnp.moveaxis(v, 2, 0)
            bT = jnp.moveaxis(beta, 2, 0)
            gT = jnp.moveaxis(gk, 2, 0)
            S0 = jnp.zeros((q.shape[0], q.shape[1], q.shape[3], v.shape[3]), q.dtype)

            def step(S, inp):
                qt, kt, vt, bt, gt = inp
                S = S * jnp.exp(gt)[..., None, None]
                u = bt[..., None] * (vt - jnp.einsum('bhk,bhkv->bhv', kt, S))
                S = S + jnp.einsum('bhk,bhv->bhkv', kt, u)
                ot = jnp.einsum('bhk,bhkv->bhv', qt, S)
                return (S, ot)
            _, o = jax.lax.scan(step, S0, (qT, kT, vT, bT, gT))
            return jnp.moveaxis(o, 0, 2)
        b, l, _ = x.shape
        xz = jnp.swapaxes(x @ W_in, 1, 2)
        xc, zc = jnp.split(xz, 2, axis=1)
        xs = jax.nn.silu(_dwconv(xc, conv_x_w, conv_x_b))
        zs = jax.nn.silu(_dwconv(zc, conv_z_w, conv_z_b))
        xs = jnp.swapaxes(xs, 1, 2)
        q = (xs @ W_q).reshape(b, l, H, DK).transpose(0, 2, 1, 3)
        k = (xs @ W_k).reshape(b, l, H, DK).transpose(0, 2, 1, 3)
        v = (xs @ W_v).reshape(b, l, H, DV).transpose(0, 2, 1, 3)
        gk = -jnp.exp(A_log) * jax.nn.softplus(xs @ W_gk + dt_bias)
        gk = jnp.swapaxes(gk, 1, 2)
        beta = jnp.swapaxes(jax.nn.sigmoid(xs @ W_b + b_b), 1, 2)
        q = _l2norm(q)
        k = _l2norm(k)
        o = _gated_delta_rule(q, k, v, beta, gk)
        o = o.transpose(0, 2, 1, 3)
        g = (xs @ W_g).reshape(b, l, H, DV)
        o = o * jax.lax.rsqrt(jnp.mean(o * o, axis=-1, keepdims=True) + EPS) * g_norm_w
        o = o * (g * jax.nn.sigmoid(g))
        o = o.reshape(b, l, VALUE_DIM)
        y = o @ W_so
        y = jnp.concatenate([y, jnp.swapaxes(zs, 1, 2)], axis=-1)
        return y @ W_out

    def _L0_xattn_ref(xx, ee, ln1_g, ln1_b, ln2_g, ln2_b, a1_wq, a1_wk, a1_wv, a1_li1_w, a1_li1_b, a1_lnx_g, a1_lnx_b, a1_lny_g, a1_lny_b, a1_ln3_g, a1_ln3_b, a1_li2_w, a1_li2_b, a1_li3_w, a1_li3_b, a2_wq, a2_wk, a2_wv, a2_li1_w, a2_li1_b, a2_lnx_g, a2_lnx_b, a2_lny_g, a2_lny_b, a2_ln3_g, a2_ln3_b, a2_li2_w, a2_li2_b, a2_li3_w, a2_li3_b, training):
        import jax, jax.numpy as jnp
        import numpy as np
        H, D, C1, C2, S, M, B, W = (16, 32, 128, 64, 256, 64, 2, 4)

        def _ln(x, g, b):
            m = jnp.mean(x, -1, keepdims=True)
            v = jnp.var(x, -1, keepdims=True)
            return (x - m) * jax.lax.rsqrt(v + 1e-05) * g + b

        def _mha(x, y, wq, wk, wv, li1_w, li1_b, lnx_g, lnx_b, lny_g, lny_b, ln3_g, ln3_b, li2_w, li2_b, li3_w, li3_b, causal):
            xn = _ln(x, lnx_g, lnx_b)
            yn = _ln(y, lny_g, lny_b)
            q = jnp.einsum('bsc,hcd->bhsd', xn, wq)
            k = jnp.einsum('btc,hcd->bhtd', yn, wk)
            v = jnp.einsum('btc,hcd->bhtd', yn, wv)
            a = jax.nn.softmax(jnp.einsum('bhsd,bhtd->bhst', q, k) * D ** (-0.5), axis=-1)
            if causal:
                s, t = (a.shape[-2], a.shape[-1])
                mask = (jnp.arange(t)[None, :] > jnp.arange(s)[:, None]).astype(a.dtype)
                a = a * mask
            o = jnp.einsum('bhst,bhtd->bhsd', a, v)
            o = o.transpose(0, 2, 1, 3).reshape(x.shape[0], x.shape[1], H * D)
            x_out = x + o @ li1_w + li1_b
            h = jax.nn.gelu(_ln(x_out, ln3_g, ln3_b) @ li2_w + li2_b, approximate=False)
            return x_out + h @ li3_w + li3_b
        x = _ln(xx, ln1_g, ln1_b)
        x = x + _mha(x, x, a1_wq, a1_wk, a1_wv, a1_li1_w, a1_li1_b, a1_lnx_g, a1_lnx_b, a1_lny_g, a1_lny_b, a1_ln3_g, a1_ln3_b, a1_li2_w, a1_li2_b, a1_li3_w, a1_li3_b, causal=True)
        x = _ln(x, ln2_g, ln2_b)
        return x + _mha(x, ee, a2_wq, a2_wk, a2_wv, a2_li1_w, a2_li1_b, a2_lnx_g, a2_lnx_b, a2_lny_g, a2_lny_b, a2_ln3_g, a2_ln3_b, a2_li2_w, a2_li2_b, a2_li3_w, a2_li3_b, causal=False)

    def _L0_ffn_ref(src, in_proj_w, in_proj_b, out_w, out_b, gate_w, gate_b, w1, b1, w2, b2, ln1_g, ln1_b, ln2_g, ln2_b):
        import jax, jax.numpy as jnp
        import numpy as np
        S, B, D, H, E, K, F = (128, 4, 128, 16, 8, 2, 512)

        def _ln(x, g, b, eps=1e-05):
            mu = jnp.mean(x, axis=-1, keepdims=True)
            var = jnp.mean((x - mu) ** 2, axis=-1, keepdims=True)
            return (x - mu) * jax.lax.rsqrt(var + eps) * g + b
        s_len, bsz, d = src.shape
        dh = d // H
        qkv = src @ in_proj_w.T + in_proj_b
        q, k, v = jnp.split(qkv, 3, axis=-1)
        q = q.reshape(s_len, bsz, H, dh)
        k = k.reshape(s_len, bsz, H, dh)
        v = v.reshape(s_len, bsz, H, dh)
        scale = dh ** (-0.5)
        scores = jnp.einsum('sbhd,tbhd->bhst', q, k) * scale
        attn = jax.nn.softmax(scores, axis=-1)
        ctx = jnp.einsum('bhst,tbhd->sbhd', attn, v).reshape(s_len, bsz, d)
        attn_out = ctx @ out_w.T + out_b
        x = _ln(src + attn_out, ln1_g, ln1_b)
        tok = x.reshape(-1, d)
        n_tok = tok.shape[0]
        logits = tok @ gate_w.T + gate_b
        probs = jax.nn.softmax(logits, axis=-1)
        topv, topi = jax.lax.top_k(probs, K)
        topv = topv / jnp.sum(topv, axis=-1, keepdims=True)
        combine = jnp.zeros_like(probs).at[jnp.arange(n_tok)[:, None], topi].set(topv)
        moe_out = jnp.zeros_like(tok)
        for e in range(E):
            h = jax.nn.relu(tok @ w1[e].T + b1[e]) @ w2[e].T + b2[e]
            moe_out = moe_out + combine[:, e:e + 1] * h
        moe_out = moe_out.reshape(s_len, bsz, d)
        return _ln(x + moe_out, ln2_g, ln2_b)

    def _L1_attn_ref(x, w_qkv, w_out, b_out):
        import jax, jax.numpy as jnp
        import numpy as np
        DIM = 128
        HEADS = 16
        SCALE = DIM ** (-0.5)
        b, n, d = x.shape
        h = HEADS
        hd = d // h
        qkv = x @ w_qkv
        qkv = qkv.reshape(b, n, 3, h, hd)
        q, k, v = (jnp.moveaxis(qkv, (2, 3), (0, 2))[i] for i in range(3))
        dots = jnp.einsum('bhid,bhjd->bhij', q, k) * SCALE
        causal_mask = jnp.triu(jnp.ones((n, n), dtype=bool), k=1)
        dots = jnp.where(causal_mask, -jnp.inf, dots)
        attn = jax.nn.softmax(dots, axis=-1)
        out = jnp.einsum('bhij,bhjd->bhid', attn, v)
        out = jnp.moveaxis(out, 1, 2).reshape(b, n, d)
        return out @ w_out + b_out

    def _L1_xattn_ref(x, weights, ensembles, proj_in, proj_out):
        import jax, jax.numpy as jnp
        import numpy as np
        E = proj_in.shape[0]
        h = jax.nn.relu(jnp.einsum('edi,bsi->bsed', proj_in, x))
        o = jnp.einsum('eid,bsed->bsei', proj_out, h)
        onehot = jax.nn.one_hot(ensembles, E, dtype=x.dtype)
        gate = jnp.einsum('bks,bkse->bse', weights, onehot)
        return jnp.einsum('bsei,bse->bsi', o, gate)

    def _L1_ffn_ref(x, Wg, W1, b1, W2, b2):
        import jax, jax.numpy as jnp
        import numpy as np
        D_MODEL, D_FF, N_EXPERTS, TOP_K = (128, 512, 8, 2)
        B = x.shape[:-1]
        xs = x.reshape(-1, x.shape[-1])
        T = xs.shape[0]
        gate_logits = xs @ Wg
        weights, sel = jax.lax.top_k(gate_logits, TOP_K)
        weights = jax.nn.softmax(weights.astype(jnp.float32), axis=1).astype(x.dtype)
        h = jax.nn.relu(jnp.einsum('td,edf->etf', xs, W1) + b1[:, None, :])
        out_e = jnp.einsum('etf,efd->etd', h, W2) + b2[:, None, :]
        tok = jnp.arange(T)
        picked = out_e[sel, tok[:, None]]
        out = jnp.einsum('tk,tkd->td', weights, picked)
        return out.reshape(*B, x.shape[-1])
    x = x + _L0_attn_ref(_layernorm(x, axis=-1), L0_attn_W_in, L0_attn_conv_x_w, L0_attn_conv_x_b, L0_attn_conv_z_w, L0_attn_conv_z_b, L0_attn_W_q, L0_attn_W_k, L0_attn_W_v, L0_attn_W_g, L0_attn_W_gk, L0_attn_W_b, L0_attn_b_b, L0_attn_A_log, L0_attn_dt_bias, L0_attn_g_norm_w, L0_attn_W_so, L0_attn_W_out)
    x = x + _L0_xattn_ref(_layernorm(x, axis=-1), ctx_512, L0_xattn_ln1_g, L0_xattn_ln1_b, L0_xattn_ln2_g, L0_xattn_ln2_b, L0_xattn_a1_wq, L0_xattn_a1_wk, L0_xattn_a1_wv, L0_xattn_a1_li1_w, L0_xattn_a1_li1_b, L0_xattn_a1_lnx_g, L0_xattn_a1_lnx_b, L0_xattn_a1_lny_g, L0_xattn_a1_lny_b, L0_xattn_a1_ln3_g, L0_xattn_a1_ln3_b, L0_xattn_a1_li2_w, L0_xattn_a1_li2_b, L0_xattn_a1_li3_w, L0_xattn_a1_li3_b, L0_xattn_a2_wq, L0_xattn_a2_wk, L0_xattn_a2_wv, L0_xattn_a2_li1_w, L0_xattn_a2_li1_b, L0_xattn_a2_lnx_g, L0_xattn_a2_lnx_b, L0_xattn_a2_lny_g, L0_xattn_a2_lny_b, L0_xattn_a2_ln3_g, L0_xattn_a2_ln3_b, L0_xattn_a2_li2_w, L0_xattn_a2_li2_b, L0_xattn_a2_li3_w, L0_xattn_a2_li3_b, 0)
    x = x + _L0_ffn_ref(_layernorm(x, axis=-1), L0_ffn_in_proj_w, L0_ffn_in_proj_b, L0_ffn_out_w, L0_ffn_out_b, L0_ffn_gate_w, L0_ffn_gate_b, L0_ffn_w1, L0_ffn_b1, L0_ffn_w2, L0_ffn_b2, L0_ffn_ln1_g, L0_ffn_ln1_b, L0_ffn_ln2_g, L0_ffn_ln2_b)
    x = x + _L1_attn_ref(_layernorm(x, axis=-1), L1_attn_w_qkv, L1_attn_w_out, L1_attn_b_out)
    x = x + _L1_xattn_ref(_layernorm(x, axis=-1), ctx_512, itok_BxS2xS_0_7, L1_xattn_proj_in, L1_xattn_proj_out)
    x = x + _L1_ffn_ref(_layernorm(x, axis=-1), L1_ffn_Wg, L1_ffn_W1, L1_ffn_b1, L1_ffn_W2, L1_ffn_b2)
    return x

_drawn_inputs = setup_inputs


def setup_inputs(seed=0):
    import zlib

    import numpy as np

    out = dict(_drawn_inputs(seed))
    spreads = {'L0_attn_conv_x_b': (0.0, 0.1),
     'L0_attn_conv_z_b': (0.0, 0.1),
     'L0_attn_b_b': (0.0, 0.8),
     'L0_attn_g_norm_w': (1.0, 0.2),
     'L0_xattn_ln1_g': (1.0, 0.2),
     'L0_xattn_ln1_b': (0.0, 0.1),
     'L0_xattn_ln2_g': (1.0, 0.2),
     'L0_xattn_ln2_b': (0.0, 0.1),
     'L0_xattn_a1_li1_b': (0.0, 0.1),
     'L0_xattn_a1_lnx_g': (1.0, 0.6),
     'L0_xattn_a1_lnx_b': (0.0, 0.8),
     'L0_xattn_a1_lny_g': (1.0, 0.6),
     'L0_xattn_a1_lny_b': (0.0, 0.8),
     'L0_xattn_a1_ln3_g': (1.0, 0.6),
     'L0_xattn_a1_ln3_b': (0.0, 0.8),
     'L0_xattn_a1_li2_b': (0.0, 0.8),
     'L0_xattn_a1_li3_b': (0.0, 0.1),
     'L0_xattn_a2_li1_b': (0.0, 0.1),
     'L0_xattn_a2_lnx_g': (1.0, 0.6),
     'L0_xattn_a2_lnx_b': (0.0, 0.8),
     'L0_xattn_a2_lny_g': (1.0, 0.6),
     'L0_xattn_a2_lny_b': (0.0, 0.8),
     'L0_xattn_a2_ln3_g': (1.0, 0.6),
     'L0_xattn_a2_ln3_b': (0.0, 0.8),
     'L0_xattn_a2_li2_b': (0.0, 0.8),
     'L0_xattn_a2_li3_b': (0.0, 0.273),
     'L0_ffn_in_proj_b': (0.0, 0.8),
     'L0_ffn_out_b': (0.0, 0.371),
     'L0_ffn_gate_b': (0.0, 0.552),
     'L0_ffn_b1': (0.0, 0.8),
     'L0_ffn_b2': (0.0, 0.531),
     'L0_ffn_ln1_g': (1.0, 0.2),
     'L0_ffn_ln1_b': (0.0, 0.315),
     'L0_ffn_ln2_g': (1.0, 0.2),
     'L0_ffn_ln2_b': (0.0, 0.342),
     'L1_ffn_b1': (0.0, 0.8),
     'L1_ffn_b2': (0.0, 0.8)}
    factors = {'L0_attn_W_gk': 2.855,
     'L0_xattn_a1_wq': 8.0,
     'L0_xattn_a1_wk': 8.0,
     'L0_xattn_a1_wv': 8.0,
     'L0_xattn_a1_li1_w': 8.0,
     'L0_xattn_a1_li2_w': 3.351,
     'L0_xattn_a1_li3_w': 3.041,
     'L0_xattn_a2_wq': 8.0,
     'L0_xattn_a2_wk': 8.0,
     'L0_xattn_a2_wv': 4.071,
     'L0_xattn_a2_li1_w': 4.082,
     'L0_xattn_a2_li2_w': 3.202,
     'L0_xattn_a2_li3_w': 2.91,
     'L0_ffn_in_proj_w': 8.0,
     'L0_ffn_out_w': 7.774,
     'L0_ffn_gate_w': 3.308,
     'L0_ffn_w1': 5.395,
     'L0_ffn_w2': 4.106,
     'L1_attn_b_out': 8.0,
     'L1_ffn_Wg': 7.201,
     'L1_ffn_W1': 8.0,
     'L1_ffn_W2': 8.0}
    for name, (base, spread) in spreads.items():
        noise = np.random.default_rng([zlib.crc32(name.encode()), seed]).standard_normal(out[name].shape)
        drawn = base * np.exp(spread * noise) if base else spread * noise
        out[name] = jnp.asarray(drawn.astype(out[name].dtype))
    for name, factor in factors.items():
        out[name] = (out[name] * factor).astype(out[name].dtype)
    return out
```

```python
from contextlib import ExitStack

import numpy as np

import concourse.bass as bass
from concourse import mybir

F32 = mybir.dt.float32
I32 = mybir.dt.int32
ALU = mybir.AluOpType
ACT = mybir.ActivationFunctionType
AX = mybir.AxisListType.X

EPS = 1e-5
NEG = -1e30


class Op:

    def __init__(self, eng, fn, waits, sem=None):
        self.eng, self.fn, self.waits, self.sem = eng, fn, waits, sem
        self.used = False
        self.n = None


class Queues:

    ENG = ("pe", "act", "dve", "pool", "sp")

    def __init__(self):
        self.q = {e: [] for e in self.ENG}

    def put(self, eng, fn, *waits, sem=None):
        flat = []

        def add(w):
            if w is None:
                return
            if isinstance(w, Op):
                w.used = True
                flat.append(w)
            else:
                for x in w:
                    add(x)

        add(waits)
        op = Op(eng, fn, flat, sem)
        self.q[eng].append(op)
        return op

    def number(self):
        for e in self.ENG:
            n = 0
            for op in self.q[e]:
                if op.sem is None and op.used:
                    n += 1
                    op.n = n

    def emit(self, eng, handle, sems):
        seen = {}
        for op in self.q[eng]:
            need = {}
            for w in op.waits:
                key = w.eng if w.sem is None else w.sem
                val = w.n if w.sem is None else 16
                if need.get(key, 0) < val:
                    need[key] = val
            for key, val in need.items():
                if seen.get(key, 0) < val:
                    seen[key] = val
                    handle.wait_ge(sems[key], val)
            ins = op.fn(handle)
            if op.sem is not None:
                ins.then_inc(sems[op.sem], 16)
            elif op.used:
                ins.then_inc(sems[eng], 1)


def columns(parts):
    at, out = 0, {}
    for name, n in parts:
        out[name] = (at, n)
        at += n
    return out, at


CST, CST_N = columns([
    ("ident", 128), ("le", 128), ("sl", 128), ("nm0", 128), ("nm1", 128), ("nm2", 128), ("nm3", 128), ("nn", 128),
    ("later", 64), ("causal", 64), ("m32", 4), ("m8", 16), ("m24", 4), ("tri", 64), ("half", 1), ("one", 1), ("eids", 8),
])
COL, COL_N = columns([
    ("cxw", 4), ("cxb", 1), ("czw", 4), ("czb", 1),
    ("a1_xg", 1), ("a1_xb", 1), ("a1_yg", 1), ("a1_yb", 1), ("a1_3g", 1), ("a1_3b", 1), ("a1_li2b", 4),
    ("a2_xg", 1), ("a2_xb", 1), ("a2_yg", 1), ("a2_yb", 1), ("a2_3g", 1), ("a2_3b", 1), ("a2_li2b", 4),
    ("ipb", 2), ("f_b1", 32), ("g_b1", 32), ("f_b2", 128), ("g_b2", 128),
])
ROW, ROW_N = columns([
    ("ln1g", 128), ("ln1b", 128), ("a1_li1b", 128), ("a1_li3b", 128), ("ln2g", 128), ("ln2b", 128),
    ("a2_li1b", 128), ("a2_li3b", 128), ("vb", 128), ("outb", 128), ("f1g", 128), ("f1b", 128), ("f2g", 128), ("f2b", 128),
    ("bout", 128), ("gnw", 48), ("dtb", 8), ("alog", 4), ("gateb", 8),
])
WA, WA_N = columns([
    ("win", 256), ("wtm", 584), ("wso", 256), ("wout", 256),
    ("a1_wq", 512), ("a1_wk", 512), ("a1_wv", 512), ("a1_li1", 512), ("a1_li2", 512), ("a1_li3", 512),
    ("a2_wq", 512), ("a2_wk", 512), ("a2_wv", 512), ("a2_li1", 512), ("a2_li2", 512), ("a2_li3", 512),
])
WS, WS_N = columns([("ip", 384), ("fo", 128), ("fg", 8), ("qkv", 384), ("lo", 128), ("wg", 8)])
WM_N = 8192
WX_N = 4096


def build(nc, x, ctx, itok, cst, col, row, wa, ws, wf, wx, wl, out):
    Q = Queues()
    put = Q.put
    es = ExitStack()
    with es:
        def sb(name, cols, dt=F32):
            return es.enter_context(nc.sbuf_tensor(name, [128, cols], dt))

        X = sb("X", 32 * 128)
        Xv = X[:, :].rearrange("p (t d) -> p t d", t=32)
        Cs = sb("Cs", CST_N)
        Cl = sb("Cl", COL_N)
        Rw = sb("Rw", ROW_N)
        R0 = sb("R0", 8192)
        Wsm = sb("Wsm", WS_N)
        EA = sb("EA", 4)
        AR_N = 35200
        AR = sb("AR", AR_N)
        PS = es.enter_context(nc.psum_tensor("PS", [128, 8, 512], F32))

        names = list(Queues.ENG)
        dma_names = []

        def c(name, a=0, b=None):
            o, n = CST[name]
            return Cs[:, o + a:o + (n if b is None else b)]

        def cl(name, j=0):
            o, n = COL[name]
            return Cl[:, o + j:o + j + 1]

        def rw(name):
            o, n = ROW[name]
            return Rw[:, o:o + n]

        def w_a(name):
            o, n = WA[name]
            return R0[:, o:o + n]

        def w_s(name):
            o, n = WS[name]
            return Wsm[:, o:o + n]

        ID = c("ident")

        def dma(dst, src, *waits):
            name = f"d{len(dma_names)}"
            dma_names.append(name)
            return put("sp", lambda e: e.dma_start(dst, src), *waits, sem=name)

        def mm(o, l, r, start, stop, *w):
            return put("pe", lambda e: e.matmul(o, l, r, start=start, stop=stop), *w)

        def tr(o, i, *w):
            n = i.shape[0]
            return put("pe", lambda e: e.transpose(o, i, ID[0:n, 0:n]), *w)

        def act(o, i, f, *w, bias=0.0, scale=1.0):
            return put("act", lambda e: e.activation(o, i, f, bias=bias, scale=scale), *w)

        def tt(eng, o, a, b, op, *w):
            return put(eng, lambda e: e.tensor_tensor(o, a, b, op), *w)

        def ts(eng, o, a, s1, s2, op0, op1, *w):
            if op1 is None:
                return put(eng, lambda e: e.tensor_scalar(o, a, s1, None, op0), *w)
            return put(eng, lambda e: e.tensor_scalar(o, a, s1, s2, op0, op1), *w)

        def stt(o, a, s, b, op0, op1, *w):
            return put("dve", lambda e: e.scalar_tensor_tensor(out=o, in0=a, scalar=s, in1=b, op0=op0, op1=op1), *w)

        def red(o, a, op, *w):
            return put("dve", lambda e: e.tensor_reduce(o, a, AX, op), *w)

        def cp(eng, o, a, *w):
            if eng == "act":
                return act(o, a, ACT.Copy, *w)
            return put(eng, lambda e: e.tensor_copy(o, a), *w)

        def bc(ap, dim, n):
            return ap.unsqueeze(dim).broadcast_to(list(ap.shape[:dim]) + [n] + list(ap.shape[dim:]))

        class Slot:

            def __init__(self, i):
                self.i = i
                self.turn = 0
                self.free = [[] for _ in range(4)]
                self.end = []
                self.base, self.size = 0, 0
                self.at = 0

            def one(self):
                b = self.turn % 4
                self.turn += 1
                return b, PS[:, 4 * self.i + b, :], self.free[b]

            def two(self):
                if self.turn % 2:
                    self.turn += 1
                b = self.turn % 4
                self.turn += 2
                p = 4 * self.i + b
                return b, PS[:, p:p + 2, :].rearrange("p a n -> p (a n)"), self.free[b] + self.free[b + 1]

            def read(self, b, tok, n=1):
                for j in range(n):
                    self.free[b + j] = [tok] if isinstance(tok, Op) else list(tok)

            def reset(self):
                self.at = self.base

            def buf(self, n):
                a = self.at
                self.at += n
                assert self.at <= self.base + self.size, (self.at - self.base, self.size)
                return AR[:, a:a + n]

        t_cst = dma(Cs[:, :], cst)
        t_x = []
        for g in range(8):
            t_x.append(dma(Xv[:, 4 * g:4 * g + 4, :], x[512 * g:512 * (g + 1), :].rearrange("(t p) d -> p t d", p=128)))
            if g == 0:
                t_col = dma(Cl[:, :], col)
                t_wa0 = dma(R0[:, 0:1352], wa[:, 0:1352])
                t_row = dma(Rw[:, :], row)
        t_wa1 = dma(R0[:, 1352:WA_N], wa[:, 1352:WA_N])
        t_ws = dma(Wsm[:, :], ws)
        t_ea = act(EA[:, :], rw("alog"), ACT.Exp, t_row)

        xw = [[t] for t in t_x]

        def stats(src, n, st, mv, rs, *w):
            last = []
            for t in range(n):
                a = put("dve", lambda e, t=t: e.bn_stats(st[:, t, :], src[:, t, :]), *w)
                last.append(a)
            ag = [put("dve", lambda e, t=t: e.bn_aggr(mv[:, t, :], st[:, t, :]), last[t]) for t in range(n)]
            a = ts("pool", rs, mv[:, :, 1], EPS, None, ALU.add, None, ag)
            half = c("half").broadcast_to([128, n])
            b = tt("pool", rs, rs, half, ALU.pow, a, t_cst)
            return ag[-1], b

        def norm(dst, src, n, mv, rs, *w, eng="dve"):
            return [ts(eng, dst[:, t, :], src[:, t, :], mv[:, t, 0:1], rs[:, t:t + 1], ALU.subtract, ALU.mult, *w)
                    for t in range(n)]

        def v3(ap, a):
            return ap.rearrange("p (a b) -> p a b", a=a)

        def flip(s, src, waits, outs):
            b, ps, fr = s.one()
            n = src.shape[2]
            for t in range(4):
                last = tr(ps[0:n, 128 * t:128 * t + 128], src[:, t, :], fr, waits[t] if len(waits) == 4 else waits, t_cst)
            done = []
            for eng, o, sc, bi, w in outs:
                if sc is None:
                    done.append(cp(eng, o, ps[0:n, :], last, w))
                elif eng == "act":
                    done.append(act(o, ps[0:n, :], ACT.Identity, last, w, t_col, done[-1:], bias=bi, scale=sc))
                else:
                    done.append(ts(eng, o, ps[0:n, :], sc, bi, ALU.mult, ALU.add, last, w, t_col, done[-1:]))
            s.read(b, done)
            return done

        class Small:
            def __init__(self, s):
                self.st = v3(s.buf(24), 4)
                self.mv = v3(s.buf(8), 4)
                self.rs = s.buf(4)

        def quad(s, g, D, qm, q_done, kF, k_done, V, v_done, B, oT, scale, mode):
            qv = qm.rearrange("p (b j s) -> p b j s", b=8, j=4)
            b, S, fr = s.two()
            for p in range(2):
                for i in range(8):
                    last = mm(S[:, p * 512 + i * 64:p * 512 + i * 64 + 64],
                              qv[:, i, 2 * p:2 * p + 2, :].rearrange("p j s -> p (j s)"),
                              kF[:, 64 * i:64 * i + 64], True, True, fr, q_done, k_done)
            B["qm_free"] = [last]
            yield
            P, mx, sm = B["P"], B["mx"], B["sm"]
            S3 = S.rearrange("p (a t) -> p a t", t=64)
            P3 = P.rearrange("p (a t) -> p a t", t=64)
            if mode == "causal":
                a = tt("dve", P3, S3, bc(c("causal"), 1, 16), ALU.add, last, B["P_free"])
                s.read(b, a, 2)
                m = red(mx, P3, ALU.max, a, B["mx_free"])
                a = tt("pool", P3, P3, bc(mx, 2, 64), ALU.subtract, m)
            else:
                m = red(mx, S3, ALU.max, last, B["mx_free"])
                a = tt("dve", P3, S3, bc(mx, 2, 64), ALU.subtract, m, B["P_free"])
                s.read(b, a, 2)
            B["mx_free"] = [a]
            yield
            e = act(P, P, ACT.Exp, a, scale=scale)
            yield
            r = red(sm, P3, ALU.add, e, B["sm_free"])
            r = put("dve", lambda e_: e_.reciprocal(sm, sm), r)
            if mode == "later":
                e = tt("pool", P3, P3, bc(c("later"), 1, 16), ALU.mult, r)
            yield
            b, T, fr = s.two()
            for i in range(8):
                last = tr(T[:, 128 * i:128 * i + 128], P[:, 128 * i:128 * i + 128], fr, e)
            B["P_free"] = [last, r]
            yield
            PT = B["PT"]
            t0 = cp("act", PT[:, 0:512], T[:, 0:512], last, B["PT_free"])
            t1 = cp("act" if g % 2 else "dve", PT[:, 512:1024], T[:, 512:1024], last, B["PT_free"])
            s.read(b, t0)
            s.read(b + 1, t1)
            yield
            b, O, fr = s.two()
            for be in range(2):
                for p in range(2):
                    for i in range(4):
                        col0 = be * 512 + (i * 2 + p) * 2 * D
                        last = mm(O[:, col0:col0 + 2 * D],
                                  PT[64 * be:64 * be + 64, p * 512 + i * 128:p * 512 + i * 128 + 128],
                                  V[64 * be:64 * be + 64, i, (4 * g + 2 * p) * D:(4 * g + 2 * p + 2) * D],
                                  True, True, fr, t0, t1, v_done)
            B["PT_free"] = [last]
            yield
            h0 = 0 if D == 32 else 4 * g
            done = []
            for be in range(2):
                for pi in range(2):
                    i0 = O[64 * pi:64 * pi + 64, be * 512:be * 512 + 16 * D].rearrange(
                        "p (i a h d) -> p i a h d", i=4, a=2, h=2)[:, :, :, pi, :]
                    o0 = oT[64 * be:64 * be + 64, :, :].rearrange(
                        "p i (h d) -> p i h d", d=D)[:, :, h0 + pi:h0 + pi + 3:2, :]
                    r0 = sm[64 * pi:64 * pi + 64, :].rearrange("p (a i e) -> p i a e", a=2, i=4)[:, :, :, be]
                    done.append(tt("dve", o0, i0, bc(r0, 3, D), ALU.mult, last, r, B["oT_free"]))
            s.read(b, done, 2)
            B["sm_free"] = done
            B["o_done"] = done
            yield

        def attn_bufs(s):
            return {"P": s.buf(1024), "mx": s.buf(16), "sm": s.buf(16), "PT": s.buf(1024),
                    "P_free": [], "mx_free": [], "sm_free": [], "PT_free": [], "qm_free": [], "oT_free": []}

        def mha(s, pf, xin, xin_done, xb, B, U, mode, ystuff):
            sm = U["small"]
            zx, zy = U["zx"], U["zy"]
            ag, rs = stats(xin, 4, sm.st, sm.mv, sm.rs, xin_done)
            yield
            nz = norm(U["z"], xin, 4, sm.mv, sm.rs, ag, rs)
            t_xb = tt("pool", xb, xin, bc(rw(pf + "_li1b"), 1, 4), ALU.add, xin_done, t_row, U["xb_free"])
            yield
            outs = [("act", zx, cl(pf + "_xg"), cl(pf + "_xb"), U["z_free"])]
            if ystuff is None:
                outs.append(("dve", zy, cl(pf + "_yg"), cl(pf + "_yb"), U["z_free"]))
            d = flip(s, U["z"], nz, outs)
            t_zx = d[0]
            if ystuff is None:
                t_zy = d[1]
                KY = 128
            else:
                yT, t_y = ystuff
                t_zy = flip(s, yT, t_y, [("act", zy[0:64, :], cl(pf + "_yg")[0:64], cl(pf + "_yb")[0:64], U["z_free"])])[0]
                KY = 64
            yield
            V = v3(U["V"], 4)
            v_done = []
            for t in range(4):
                b, ps, fr = s.one()
                m = mm(ps, zy[0:KY, 128 * t:128 * t + 128], w_a(pf + "_wv")[0:KY, :], True, True, fr, t_zy, t_wa1)
                v_done.append(cp("act" if t % 2 else "dve", V[:, t, :], ps, m))
                s.read(b, v_done[-1])
            yield
            k_free, oF_done = [], []
            for g in range(4):
                b, ps, fr = s.one()
                m = mm(ps, w_a(pf + "_wq")[:, 128 * g:128 * g + 128], zx, True, True, fr, t_zx, t_wa1)
                qv = U["qm"].rearrange("p (b j s) -> p b j s", b=8, j=4)
                q_done = []
                for j in range(4):
                    i0 = ps.rearrange("p (b s) -> p b s", b=8)
                    if g % 2:
                        q_done.append(act(qv[:, :, j, :], i0, ACT.Copy, m, B["qm_free"], scale=c("m32", j, j + 1)))
                    else:
                        q_done.append(ts("dve", qv[:, :, j, :], i0, c("m32", j, j + 1), None, ALU.mult, None, m, B["qm_free"]))
                s.read(b, q_done)
                b, ps, fr = s.one()
                m = mm(ps, w_a(pf + "_wk")[0:KY, 128 * g:128 * g + 128], zy[0:KY, :], True, True, fr, t_zy)
                k_done = cp("act", U["kF"], ps, m, B["qm_free"])
                s.read(b, k_done)
                yield
                oT = U["oT"]
                yield from quad(s, g, 32, U["qm"], q_done, U["kF"], k_done, V, v_done, B, oT, 32 ** -0.5, mode)
                b, ps, fr = s.one()
                for t in range(4):
                    m = tr(ps[:, 128 * t:128 * t + 128], oT[:, t, :], fr, B["o_done"])
                B["oT_free"] = [m]
                yield
                oF_done.append(cp("act", U["oF"][:, 512 * g:512 * g + 512], ps, m))
                s.read(b, oF_done[-1])
                yield
            b, ps, fr = s.one()
            for t in range(4):
                for g in range(4):
                    m = mm(ps[:, 128 * t:128 * t + 128], U["oF"][:, 512 * g + 128 * t:512 * g + 128 * t + 128],
                           w_a(pf + "_li1")[:, 128 * g:128 * g + 128], g == 0, g == 3, fr, oF_done)
            yield
            xo = U["xo"]
            t_xo = tt("dve", xo, v3(ps, 4), xb, ALU.add, m, t_xb, U["xo_free"])
            s.read(b, t_xo)
            ag, rs = stats(xo, 4, sm.st, sm.mv, sm.rs, t_xo, nz)
            yield
            nz = norm(U["z"], xo, 4, sm.mv, sm.rs, ag, rs)
            t_r = tt("pool", xb, xin, bc(rw(pf + "_li3b"), 1, 4), ALU.add, t_xo)
            t_r = tt("pool", xb, xb, xo, ALU.add, t_r)
            yield
            t_zx = flip(s, U["z"], nz, [("act", zx, cl(pf + "_3g"), cl(pf + "_3b"), [])])[0]
            yield
            h = U["oF"]
            h_done = []
            for f in range(4):
                b, ps, fr = s.one()
                mh = mm(ps, w_a(pf + "_li2")[:, 128 * f:128 * f + 128], zx, True, True, fr, t_zx)
                h_done.append(act(h[:, 512 * f:512 * f + 512], ps, ACT.Gelu, mh, m, bias=cl(pf + "_li2b", f)))
                s.read(b, h_done[-1])
            yield
            b, ps, fr = s.one()
            for t in range(4):
                for f in range(4):
                    m = mm(ps[:, 128 * t:128 * t + 128], h[:, 512 * f + 128 * t:512 * f + 128 * t + 128],
                           w_a(pf + "_li3")[:, 128 * f:128 * f + 128], f == 0, f == 3, fr, h_done)
            yield
            U["res"] = (b, ps, m, t_r)

        def delta(s, G):
            s.reset()
            end = s.end
            sm = Small(s)
            xn = v3(s.buf(512), 4)
            xF = s.buf(512)
            pad = [v3(s.buf(8 * 68), 8) for _ in range(2)]
            cv = [s.buf(512) for _ in range(2)]
            TMP = s.buf(4 * 288)
            qk = v3(TMP, 4)
            vg = v3(s.buf(4 * 392), 4)
            bv = v3(s.buf(4 * 192), 4)
            kq = s.buf(1024)
            km = s.buf(2048)
            sc = s.buf(32)
            be4, g4, e8 = v3(s.buf(16), 4), v3(s.buf(16), 4), v3(s.buf(32), 4)
            rn = s.buf(32)
            AT = [s.buf(512) for _ in range(2)]
            MT = [s.buf(512) for _ in range(2)]
            XX = [s.buf(512) for _ in range(2)]
            XT = [s.buf(512) for _ in range(2)]
            PP = [s.buf(512) for _ in range(2)]
            ET = [s.buf(512) for _ in range(2)]
            UU = [s.buf(192) for _ in range(2)]
            RR = [s.buf(192) for _ in range(2)]
            o = v3(s.buf(4 * 192), 4)
            sq = o
            sq_o = v3(km[:, 0:768], 4)
            oF = kq
            yF = cv[0]
            xi = Xv[:, 4 * G:4 * G + 4, :]

            ag, rs = stats(xi, 4, sm.st, sm.mv, sm.rs, xw[G], end)
            yield
            nz = norm(xn, xi, 4, sm.mv, sm.rs, ag, rs)
            z0 = []
            for i in range(2):
                z0.append(put("pool", lambda e, i=i: e.memset(pad[i][:, :, 0:1], 0.0), end))
                z0.append(put("pool", lambda e, i=i: e.memset(pad[i][:, :, 65:67], 0.0), end))
            yield
            t_xF = flip(s, xn, nz, [("act", xF, None, None, [])])[0]
            yield
            c_done = []
            for i in range(2):
                b, ps, fr = s.one()
                m = mm(ps, w_a("win")[:, 128 * i:128 * i + 128], xF, True, True, fr, t_xF, t_wa0)
                ev = cp("act", pad[i][:, :, 1:65], ps.rearrange("p (b s) -> p b s", b=8), m)
                s.read(b, ev)
                wn, bn = ("cxw", "cxb") if i == 0 else ("czw", "czb")
                o3 = v3(cv[i], 8)
                a = ts("dve", o3, pad[i][:, :, 0:64], cl(wn, 0), cl(bn), ALU.mult, ALU.add, ev, z0, t_col)
                for j in range(1, 4):
                    a = stt(o3, pad[i][:, :, j:j + 64], cl(wn, j), o3, ALU.mult, ALU.add, a)
                c_done.append(a)
                yield
            s_done = [act(cv[i], cv[i], ACT.Silu, c_done[i]) for i in range(2)]
            yield
            xs = cv[0]
            wt = w_a("wtm")
            e_vg, e_qk = [], []
            for t in range(4):
                b, ps, fr = s.one()
                m = mm(ps[:, 0:392], xs[:, 128 * t:128 * t + 128], wt[:, 0:392], True, True, fr, s_done)
                e_vg.append(cp("dve", vg[:, t, :], ps[:, 0:392], m))
                s.read(b, e_vg[-1])
                b, ps, fr = s.one()
                m = mm(ps[:, 0:192], xs[:, 128 * t:128 * t + 128], wt[:, 392:584], True, True, fr, s_done)
                e_qk.append(cp("act", qk[:, t, 0:192], ps[:, 0:192], m))
                s.read(b, e_qk[-1])
                if t % 2:
                    yield
            t_sg = act(vg[:, :, 192:384], vg[:, :, 192:384], ACT.Silu, e_vg)
            sq2 = sq[:, :, 0:192]
            a = tt("pool", sq2, qk[:, :, 0:192], qk[:, :, 0:192], ALU.mult, e_qk)
            yield
            rn4 = v3(rn, 4)
            a = red(rn4, sq2.rearrange("p t (h d) -> p t h d", d=24), ALU.add, a)
            a = ts("pool", rn, rn, 1e-6, None, ALU.add, None, a)
            a = tt("pool", rn, rn, c("half").broadcast_to([128, 32]), ALU.pow, a)
            a_n = [tt("pool", qk[:, t, 0:192].rearrange("p (h d) -> p h d", d=24), qk[:, t, 0:192].rearrange("p (h d) -> p h d", d=24),
                      bc(rn4[:, t, :], 2, 24), ALU.mult, a) for t in range(4)]
            p8 = tt("dve", e8, vg[:, :, 384:392], bc(rw("dtb"), 1, 4), ALU.add, e_vg, t_row)
            ab = stt(g4, e8[:, :, 0:4], -1.0, e8[:, :, 0:4], ALU.mult, ALU.min, p8)
            yield
            e1 = act(be4, e8[:, :, 4:8], ACT.Exp, p8, scale=-1.0)
            e2 = act(g4, g4, ACT.Exp, ab)
            e2 = act(g4, g4, ACT.Ln, e2, bias=1.0)
            yield
            a = ts("dve", be4, be4, 1.0, None, ALU.add, None, e1)
            t_be = put("dve", lambda e: e.reciprocal(be4, be4), a)
            a = stt(g4, e8[:, :, 0:4], 0.0, g4, ALU.max, ALU.add, e2)
            t_g = stt(g4, g4, -1.0, bc(EA[:, :], 1, 4), ALU.mult, ALU.mult, a, t_ea)
            t_kb = [tt("pool", qk[:, t, 192:288].rearrange("p (h d) -> p h d", d=24), qk[:, t, 96:192].rearrange("p (h d) -> p h d", d=24),
                       bc(be4[:, t, :], 2, 24), ALU.mult, a_n, t_be) for t in range(4)]
            t_bv = [tt("pool", bv[:, t, :].rearrange("p (h d) -> p h d", d=48), vg[:, t, 0:192].rearrange("p (h d) -> p h d", d=48),
                       bc(be4[:, t, :], 2, 48), ALU.mult, e_vg, t_be) for t in range(4)]
            yield
            kqv = kq.rearrange("p (t a s) -> p t a s", t=4, a=2)
            kmv = km.rearrange("p (t h s) -> p t h s", t=4, h=4)
            kq_done = []
            for slot_i, off, eng in ((0, 192, "act"), (1, 0, "dve")):
                b, ps, fr = s.one()
                for t in range(4):
                    m = tr(ps[0:96, 128 * t:128 * t + 128], qk[:, t, off:off + 96], fr, t_kb, a_n)
                kq_done.append(cp(eng, kqv[0:96, :, slot_i, :], v3(ps, 4)[0:96], m))
                s.read(b, kq_done[-1])
            b, ps, fr = s.one()
            for t in range(4):
                m = tr(ps[0:96, 128 * t:128 * t + 128], qk[:, t, 96:192], fr, a_n)
            km_done = []
            for h in range(4):
                o_, i_, s_ = kmv[0:96, :, h, :], v3(ps, 4)[0:96], c("m24", h, h + 1)[0:96]
                if G % 2:
                    km_done.append(act(o_, i_, ACT.Copy, m, scale=s_))
                else:
                    km_done.append(ts("dve", o_, i_, s_, None, ALU.mult, None, m))
            s.read(b, km_done)
            yield
            o_done = []
            ufree = []
            for half in range(2):
                tl = [2 * half, 2 * half + 1]
                W = {}
                for i, t in enumerate(tl):
                    GR = v3(PP[i], 4)
                    gr = [ts("pool", GR[:, h, :], c("sl"), g4[:, t, h:h + 1], None, ALU.mult, None, t_g, ufree) for h in range(4)]
                    b, ps, fr = s.one()
                    for h in range(4):
                        m = mm(ps[:, 128 * h:128 * h + 128], GR[:, h, :], c("le"), True, True, fr, gr)
                    W["dt", i] = m
                    ex = act(ET[i], ps, ACT.Exp, m, ufree)
                    s.read(b, ex)
                    W["et", i] = tt("pool", v3(ET[i], 4), v3(ET[i], 4), bc(c("le"), 1, 4), ALU.mult, ex)
                yield
                for i, t in enumerate(tl):
                    b, ps, fr = s.two()
                    for h in range(4):
                        m = mm(ps[:, 256 * h:256 * h + 256], kmv[0:96, t, h, :], kqv[0:96, t, :, :].rearrange("p a s -> p (a s)"),
                               True, True, fr, km_done, kq_done)
                    pv = ps.rearrange("p (h a s) -> p h a s", h=4, a=2)
                    a1 = tt("dve", v3(AT[i], 4), pv[:, :, 0, :], v3(ET[i], 4), ALU.mult, m, W["et", i], ufree)
                    a2 = tt("dve", v3(MT[i], 4), pv[:, :, 1, :], v3(ET[i], 4), ALU.mult, m, W["et", i], ufree)
                    s.read(b, [a1, a2], 2)
                    W["at", i], W["mt", i] = a1, a2
                yield
                for i, t in enumerate(tl):
                    a = tt("pool", v3(XT[i], 4), v3(AT[i], 4), bc(c("nm0"), 1, 4), ALU.mult, W["at", i], ufree)
                    a = tt("pool", v3(XT[i], 4), v3(XT[i], 4), bc(ID, 1, 4), ALU.add, a)
                    b, ps, fr = s.one()
                    for h in range(4):
                        m = tr(ps[:, 128 * h:128 * h + 128], XT[i][:, 128 * h:128 * h + 128], fr, a)
                    W["xt", i] = a
                    W["x", i] = cp("act", XX[i], ps, m, ufree)
                    s.read(b, W["x", i])
                yield
                for lv in range(1, 4):
                    for i, t in enumerate(tl):
                        prev = W.get(("pm", i))
                        ak = tt("pool", v3(ET[i], 4), v3(AT[i], 4), bc(c(f"nm{lv}"), 1, 4), ALU.mult, W["at", i], W["mt", i], prev)
                        b, ps, fr = s.one()
                        for h in range(4):
                            sl_ = slice(128 * h, 128 * h + 128)
                            m = mm(ps[:, sl_], ET[i][:, sl_], XX[i][:, sl_], True, True, fr, ak, W["x", i])
                        W["pm", i] = m
                        W["p", i] = cp("act", PP[i], ps, m, W["dt", i], W.get(("pr", i)))
                        s.read(b, W["p", i])
                    yield
                    for i, t in enumerate(tl):
                        b, ps, fr = s.one()
                        for h in range(4):
                            sl_ = slice(128 * h, 128 * h + 128)
                            if lv < 3:
                                m = mm(ps[:, sl_], XT[i][:, sl_], PP[i][:, sl_], True, True, fr, W["p", i], W["xt", i])
                            else:
                                m = mm(ps[:, sl_], PP[i][:, sl_], XT[i][:, sl_], True, True, fr, W["p", i], W["xt", i])
                        W["pr", i] = m
                        if lv < 3:
                            W["x", i] = tt("dve", XX[i], ps, XX[i], ALU.add, m)
                            s.read(b, W["x", i])
                            b, ps, fr = s.one()
                            for h in range(4):
                                m = tr(ps[:, 128 * h:128 * h + 128], XX[i][:, 128 * h:128 * h + 128], fr, W["x", i])
                            W["xt", i] = cp("act", XT[i], ps, m)
                            s.read(b, W["xt", i])
                        else:
                            W["xt", i] = tt("dve", XT[i], ps, XT[i], ALU.add, m)
                            s.read(b, W["xt", i])
                    yield
                for i, t in enumerate(tl):
                    W["nn", i] = tt("pool", v3(ET[i], 4), v3(AT[i], 4), bc(c("nn"), 1, 4), ALU.mult, W["pm", i])
                    W["r", i] = t_bv[t]
                for it in range(4):
                    for i, t in enumerate(tl):
                        src = bv[:, t, :] if it == 0 else RR[i]
                        b, ps, fr = s.one()
                        for h in range(4):
                            m = mm(ps[:, 48 * h:48 * h + 48], XT[i][:, 128 * h:128 * h + 128], src[:, 48 * h:48 * h + 48],
                                   True, True, fr, W["r", i], W["xt", i])
                        W["u", i] = cp("act", UU[i], ps[:, 0:192], m, ufree if it == 0 else W["um", i])
                        s.read(b, W["u", i])
                        W["rm", i] = m
                    yield
                    if it == 3:
                        break
                    for i, t in enumerate(tl):
                        b, ps, fr = s.one()
                        for h in range(4):
                            m = mm(ps[:, 48 * h:48 * h + 48], ET[i][:, 128 * h:128 * h + 128], UU[i][:, 48 * h:48 * h + 48],
                                   True, True, fr, W["u", i], W["nn", i])
                        W["um", i] = m
                        W["r", i] = tt("dve", RR[i], ps[:, 0:192], bv[:, t, :], ALU.add, m, W["rm", i])
                        s.read(b, W["r", i])
                    yield
                for i, t in enumerate(tl):
                    b, ps, fr = s.one()
                    for h in range(4):
                        m = mm(ps[:, 48 * h:48 * h + 48], MT[i][:, 128 * h:128 * h + 128], UU[i][:, 48 * h:48 * h + 48],
                               True, True, fr, W["u", i], W["mt", i])
                    o_done.append(cp("act", o[:, t, :], ps[:, 0:192], m))
                    s.read(b, o_done[-1])
                ufree = list(o_done)
                yield
            a = tt("pool", sq_o, o, o, ALU.mult, o_done, t_kb)
            a = red(v3(rn[:, 0:16], 4), sq_o.rearrange("p t (h d) -> p t h d", d=48), ALU.add, a, t_kb)
            a = ts("pool", rn[:, 0:16], rn[:, 0:16], 1.0 / 48, EPS, ALU.mult, ALU.add, a)
            a = tt("pool", rn[:, 0:16], rn[:, 0:16], c("half").broadcast_to([128, 16]), ALU.pow, a)
            yield
            o16 = o.rearrange("p t (h d) -> p (t h) d", d=48)
            a = tt("pool", o16, o16, bc(rn[:, 0:16], 2, 48), ALU.mult, a)
            a = tt("dve", o16, o16, bc(rw("gnw"), 1, 16), ALU.mult, a)
            a = tt("dve", o, o, vg[:, :, 192:384], ALU.mult, a, t_sg)
            yield
            b, ps, fr = s.one()
            for t in range(4):
                m = tr(ps[:, 128 * t:128 * t + 128], o[:, t, 0:128], fr, a)
            f0 = cp("act", oF[:, 0:512], ps, m)
            s.read(b, f0)
            b, ps, fr = s.one()
            for t in range(4):
                m = tr(ps[0:64, 128 * t:128 * t + 128], o[:, t, 128:192], fr, a)
            f1 = cp("act", oF[0:64, 512:1024], ps[0:64, :], m)
            s.read(b, f1)
            yield
            b, ps, fr = s.one()
            mm(ps, w_a("wso")[:, 0:128], oF[:, 0:512], True, False, fr, f0)
            m = mm(ps, w_a("wso")[0:64, 128:256], oF[0:64, 512:1024], False, True, f1)
            y = cp("act", yF, ps, m, e_vg, e_qk)
            s.read(b, y)
            yield
            b, ps, fr = s.one()
            for t in range(4):
                mm(ps[:, 128 * t:128 * t + 128], yF[:, 128 * t:128 * t + 128], w_a("wout")[:, 0:128], True, False, fr, y)
                m = mm(ps[:, 128 * t:128 * t + 128], cv[1][:, 128 * t:128 * t + 128], w_a("wout")[:, 128:256], False, True, s_done)
            a = tt("dve", xi, v3(ps, 4), xi, ALU.add, m)
            s.read(b, a)
            xw[G] = [a]
            s.end = [a]
            yield

        def xattn(s, G):
            s.reset()
            end = s.end
            sm = Small(s)
            sm2 = Small(s)
            x1 = v3(s.buf(512), 4)
            x3 = v3(s.buf(512), 4)
            eT = v3(s.buf(256), 4)
            U = {"small": sm, "z": v3(s.buf(512), 4), "zx": s.buf(512), "zy": s.buf(512), "V": s.buf(2048),
                 "qm": s.buf(2048), "kF": s.buf(512), "oT": v3(s.buf(512), 4), "oF": s.buf(2048),
                 "xo": v3(s.buf(512), 4), "z_free": [], "xb_free": [], "xo_free": []}
            xb = v3(s.buf(512), 4)
            B = attn_bufs(s)
            xi = Xv[:, 4 * G:4 * G + 4, :]
            t_e = dma(eT, ctx[512 * G:512 * (G + 1), :].rearrange("(t p) d -> p t d", p=128), end)
            ag, rs = stats(xi, 4, sm.st, sm.mv, sm.rs, xw[G], end)
            r2 = s.buf(4)
            a = tt("pool", r2, sm.rs, sm.rs, ALU.mult, rs, end)
            a = tt("pool", r2, r2, sm.mv[:, :, 1], ALU.mult, a)
            a = ts("pool", r2, r2, EPS, None, ALU.add, None, a)
            a = tt("pool", r2, r2, c("half").broadcast_to([128, 4]), ALU.pow, a)
            a = tt("pool", sm.rs, sm.rs, r2, ALU.mult, a)
            yield
            nz = norm(x1, xi, 4, sm.mv, sm.rs, ag, a)
            a = tt("pool", x1, x1, bc(rw("ln1g"), 1, 4), ALU.mult, nz, t_row)
            a = tt("pool", x1, x1, bc(rw("ln1b"), 1, 4), ALU.add, a)
            ag2, rs2 = stats(eT, 4, sm2.st, sm2.mv, sm2.rs, t_e, end)
            ne = norm(eT, eT, 4, sm2.mv, sm2.rs, ag2, rs2)
            yield
            yield from mha(s, "a1", x1, a, xb, B, U, "later", None)
            b, ps, m, t_r = U["res"]
            a = tt("dve", xb, v3(ps, 4), xb, ALU.add, m, t_r)
            s.read(b, a)
            ag, rs = stats(xb, 4, sm.st, sm.mv, sm.rs, a)
            yield
            nz = norm(x3, xb, 4, sm.mv, sm.rs, ag, rs)
            a = tt("pool", x3, x3, bc(rw("ln2g"), 1, 4), ALU.mult, nz)
            a = tt("pool", x3, x3, bc(rw("ln2b"), 1, 4), ALU.add, a)
            yield
            yield from mha(s, "a2", x3, a, xb, B, U, "full", (eT, ne))
            b, ps, m, t_r = U["res"]
            a = tt("pool", xb, xb, xi, ALU.add, t_r)
            a = tt("dve", xi, v3(ps, 4), xb, ALU.add, m, a)
            s.read(b, a)
            xw[G] = [a]
            s.end = [a]
            yield

        def small_attn(s, src, src_done, wqkv, qb, kb, vb, mode, waits, N):
            qF, kF, V, qm, oT, B = N["qF"], N["kF"], v3(N["V"], 4), N["qm"], N["oT"], N["B"]
            b, ps, fr = s.one()
            m = mm(ps, wqkv[:, 0:128], src, True, True, fr, src_done, waits)
            if qb is None:
                tq = cp("act", qF, ps, m)
            else:
                tq = act(qF, ps, ACT.Identity, m, bias=qb)
            s.read(b, tq)
            b, ps, fr = s.one()
            m = mm(ps, wqkv[:, 128:256], src, True, True, fr, src_done)
            if kb is None:
                tk = cp("dve", kF, ps, m)
            else:
                tk = ts("dve", kF, ps, kb, None, ALU.add, None, m)
            s.read(b, tk)
            yield
            b, ps, fr = s.one()
            for t in range(4):
                m = mm(ps[:, 128 * t:128 * t + 128], src[:, 128 * t:128 * t + 128], wqkv[:, 256:384], True, True, fr)
            if vb is None:
                tv = cp("act", N["V"], ps, m)
            else:
                tv = tt("dve", V, v3(ps, 4), bc(vb, 1, 4), ALU.add, m)
            s.read(b, tv)
            yield
            done = []
            for g in range(4):
                qv = qm.rearrange("p (b j s) -> p b j s", b=8, j=4)
                qd = []
                for j in range(4):
                    i0 = qF.rearrange("p (b s) -> p b s", b=8)
                    eng = "pool" if j < 2 else "dve"
                    qd.append(ts(eng, qv[:, :, j, :], i0, c("m8", 4 * g + j, 4 * g + j + 1), None, ALU.mult, None, tq, B["qm_free"]))
                yield
                yield from quad(s, g, 8, qm, qd, kF, tk, V, tv, B, oT, N["scale"], mode)
                done += B["o_done"]
            b, ps, fr = s.one()
            for t in range(4):
                m = tr(ps[:, 128 * t:128 * t + 128], oT[:, t, :], fr, done)
            N["o"] = (b, ps, m)
            yield

        def small_bufs(s, scale):
            return {"qF": s.buf(512), "kF": s.buf(512), "V": s.buf(512), "qm": s.buf(2048), "oT": v3(s.buf(512), 4),
                    "B": attn_bufs(s), "scale": scale}

        def gates(s, lg, gt, waits, cmp, aux, n):
            c4 = cmp.rearrange("p (t e f) -> p t e f", t=n, e=8)
            tri = c("tri").rearrange("p (e f) -> p e f", e=8)
            rk = v3(aux[:, 0:8 * n], n)
            mx, sm = aux[:, 8 * n:9 * n], aux[:, 9 * n:10 * n]
            last = []
            for t in range(n):
                lf = bc(lg[:, t, :], 1, 8)
                le_ = bc(lg[:, t, :], 2, 8)
                a = tt("dve", c4[:, t], lf, le_, ALU.is_equal, waits)
                a = tt("dve", c4[:, t], c4[:, t], tri, ALU.mult, a)
                b = tt("dve", cmp2(s)[:, t], lf, le_, ALU.is_gt, waits)
                last.append(tt("dve", c4[:, t], c4[:, t], cmp2(s)[:, t], ALU.add, a, b))
            a = red(rk, c4, ALU.add, last)
            a = ts("dve", rk, rk, 1.5, None, ALU.is_lt, None, a)
            m = red(mx, lg, ALU.max, waits)
            b = tt("dve", gt, lg, bc(mx, 2, 8), ALU.subtract, m)
            e = act(gt, gt, ACT.Exp, b)
            e = tt("dve", gt, gt, rk, ALU.mult, e, a)
            r = red(sm, gt, ALU.add, e)
            r = put("dve", lambda h: h.reciprocal(sm, sm), r)
            return tt("dve", gt, gt, bc(sm, 2, 8), ALU.mult, r)

        def cmp2(s):
            return s.cmp2

        def experts(s, tF, t_done, gt, g_done, W, t_w, b1, b2, acc, acc_done, hb, gT, nf, end):
            nh = len(hb)
            w1 = W[0].rearrange("p (e f) -> p e f", e=8)
            w2 = W[1].rearrange("p (e f d) -> p e f d", e=8, f=nf)
            if b2 is not None:
                b, ps, fr = s.one()
                for t in range(4):
                    m = tr(ps[0:8, 128 * t:128 * t + 128], gt[:, t, :], fr, g_done)
                a = cp("act", gT[0:8, :], ps[0:8, :], m, end)
                s.read(b, a)
                b, ps, fr = s.one()
                for t in range(4):
                    m = mm(ps[:, 128 * t:128 * t + 128], gT[0:8, 128 * t:128 * t + 128], b2[0:8, :], True, True, fr, a)
                acc_done = tt("dve", acc, v3(ps, 4), acc, ALU.add, m, acc_done)
                s.read(b, acc_done)
                yield
            acc_t = [acc_done] * 4
            hfree = [[] for _ in range(nh)]
            pend = None

            def second(e, hd):
                h = hb[e % nh]
                b, ps, fr = s.one()
                for t in range(4):
                    for f in range(nf):
                        m = mm(ps[:, 128 * t:128 * t + 128], h[:, 512 * f + 128 * t:512 * f + 128 * t + 128],
                               w2[:, e, f, :], f == 0, f == nf - 1, fr, hd)
                hfree[e % nh] = [m]
                for t in range(4):
                    acc_t[t] = stt(acc[:, t, :], ps[:, 128 * t:128 * t + 128], gt[:, t, e:e + 1], acc[:, t, :],
                                   ALU.mult, ALU.add, m, g_done, acc_t[t])
                s.read(b, list(acc_t))

            for e in range(8):
                hd = []
                for f in range(nf):
                    b, ps, fr = s.one()
                    m = mm(ps, w1[:, e, 128 * f:128 * f + 128], tF, True, True, fr, t_done, t_w)
                    o = hb[e % nh][:, 512 * f:512 * f + 512]
                    bi = b1[:, nf * e + f:nf * e + f + 1] if b1 is not None else 0.0
                    if f % 4 == 3:
                        a = ts("dve", o, ps, bi, 0.0, ALU.add, ALU.max, m, hfree[e % nh])
                    else:
                        a = act(o, ps, ACT.Relu, m, hfree[e % nh], bias=bi)
                    s.read(b, a)
                    hd.append(a)
                    if f % 2:
                        yield
                if pend is not None:
                    second(*pend)
                    yield
                pend = (e, hd)
            second(*pend)
            yield
            return list(acc_t)

        slots = [Slot(0), Slot(1)]

        def sweep(gen, size, base):
            for i, s in enumerate(slots):
                s.base, s.size = base + i * size, size
            todo = list(range(8))
            live = [None, None]
            first = [True, True]
            while todo or any(live):
                for i in range(2):
                    if live[i] is None and todo:
                        live[i] = gen(slots[i], todo.pop(0))
                        if i == 0 and first[0]:
                            first[0] = False
                            for _ in range(LEAD):
                                next(live[0])
                    if live[i] is not None:
                        try:
                            next(live[i])
                        except StopIteration:
                            live[i] = None

        def join():
            both = slots[0].end + slots[1].end
            for s in slots:
                s.end = list(both)
            return both

        LEAD = 3

        def phase1(s, G):
            yield from delta(s, G)
            yield from xattn(s, G)

        sweep(phase1, AR_N // 2, 0)
        ph1 = join()

        WM = AR[:, 0:8192]
        WX = AR[:, 8192:12288]
        CF = AR[:, 12288:16384]
        SF = WX
        t_wf = dma(WM, wf, ph1)
        t_wl = dma(R0[:, :], wl, ph1)
        s_base = 16384
        s_size = (AR_N - s_base) // 2

        sf_done = []

        def turn(s, G):
            s.reset()
            sm = Small(s)
            z = v3(s.buf(512), 4)
            xi = Xv[:, 4 * G:4 * G + 4, :]
            ag, rs = stats(xi, 4, sm.st, sm.mv, sm.rs, xw[G], s.end)
            yield
            nz = norm(z, xi, 4, sm.mv, sm.rs, ag, rs)
            b, ps, fr = s.one()
            for t in range(4):
                m = tr(ps[:, 128 * t:128 * t + 128], z[:, t, :], fr, nz[t])
            yield
            o = SF.rearrange("p (j i) -> p i j", i=64)[:, 8 * G:8 * G + 8, :]
            a = cp("act" if G % 2 else "dve", o, ps.rearrange("p (i j) -> p i j", i=8), m)
            s.read(b, a)
            sf_done.append(a)
            s.end = [a]
            yield

        sweep(turn, s_size, s_base)
        join()
        cf_done = []

        def across(s, G):
            s.reset()
            N = small_bufs(s, 8 ** -0.5)
            src = SF[:, 512 * G:512 * G + 512]
            wait = [sf_done, s.end, t_ws]
            yield from small_attn(s, src, sf_done, w_s("ip"), cl("ipb", 0), cl("ipb", 1), rw("vb"), "full", wait, N)
            b, ps, m = N["o"]
            o = CF.rearrange("p (i j) -> p j i", j=64)[:, 8 * G:8 * G + 8, :]
            a = cp("act", o, ps.rearrange("p (j i) -> p j i", j=8), m)
            s.read(b, a)
            cf_done.append(a)
            s.end = [a]
            yield

        sweep(across, s_size, s_base)
        ph2 = join()
        t_wx = dma(WX, wx, ph2)

        def moe_bufs(s):
            s.cmp2 = s.buf(256).rearrange("p (t e f) -> p t e f", t=4, e=8)
            return {"small": Small(s), "z": v3(s.buf(512), 4), "x": v3(s.buf(512), 4), "xF": s.buf(512),
                    "cmp": s.buf(256), "aux": s.buf(40), "lg": v3(s.buf(32), 4), "gt": v3(s.buf(32), 4),
                    "h": [s.buf(2048) for _ in range(2)], "gT": s.buf(512)}

        def ffn0(s, G):
            s.reset()
            U = moe_bufs(s)
            sm = U["small"]
            xi = Xv[:, 4 * G:4 * G + 4, :]
            end = s.end
            ag, rs = stats(xi, 4, sm.st, sm.mv, sm.rs, xw[G], end)
            b, ps, fr = s.one()
            for t in range(4):
                m = mm(ps[:, 128 * t:128 * t + 128], CF[:, 512 * G + 128 * t:512 * G + 128 * t + 128], w_s("fo"), True, True, fr, cf_done, t_ws)
            yield
            z, x1 = U["z"], U["x"]
            nz = norm(z, xi, 4, sm.mv, sm.rs, ag, rs)
            a = tt("pool", z, z, bc(rw("outb"), 1, 4), ALU.add, nz)
            a = tt("dve", z, v3(ps, 4), z, ALU.add, m, a)
            s.read(b, a)
            ag, rs = stats(z, 4, sm.st, sm.mv, sm.rs, a)
            yield
            nz = norm(x1, z, 4, sm.mv, sm.rs, ag, rs)
            a = tt("pool", x1, x1, bc(rw("f1g"), 1, 4), ALU.mult, nz)
            a = tt("pool", x1, x1, bc(rw("f1b"), 1, 4), ALU.add, a)
            yield
            t_F = flip(s, x1, [a], [("act", U["xF"], None, None, [])])[0]
            yield
            b, ps, fr = s.one()
            for t in range(4):
                m = mm(ps[:, 8 * t:8 * t + 8], U["xF"][:, 128 * t:128 * t + 128], w_s("fg"), True, True, fr, t_F)
            l = tt("dve", U["lg"], v3(ps[:, 0:32], 4), bc(rw("gateb"), 1, 4), ALU.add, m)
            s.read(b, l)
            gd = gates(s, U["lg"], U["gt"], [l], U["cmp"], U["aux"], 4)
            yield
            o, n = COL["f_b1"]
            o2, n2 = COL["f_b2"]
            fin = yield from experts(s, U["xF"], t_F, U["gt"], gd, (WM[:, 0:4096], WM[:, 4096:8192]), t_wf,
                                     Cl[:, o:o + n], Cl[:, o2:o2 + n2], x1, a, U["h"], U["gT"], 4, end)
            ag, rs = stats(x1, 4, sm.st, sm.mv, sm.rs, fin)
            yield
            nz = norm(x1, x1, 4, sm.mv, sm.rs, ag, rs)
            a = tt("pool", x1, x1, bc(rw("f2g"), 1, 4), ALU.mult, nz)
            a = tt("pool", x1, x1, bc(rw("f2b"), 1, 4), ALU.add, a)
            a = tt("dve", xi, xi, x1, ALU.add, a)
            xw[G] = [a]
            s.end = [a]
            yield

        def attn1(s, G):
            s.reset()
            sm = Small(s)
            z, zF, oF = v3(s.buf(512), 4), s.buf(512), s.buf(512)
            N = small_bufs(s, 128 ** -0.5)
            xi = Xv[:, 4 * G:4 * G + 4, :]
            ag, rs = stats(xi, 4, sm.st, sm.mv, sm.rs, xw[G], s.end)
            yield
            nz = norm(z, xi, 4, sm.mv, sm.rs, ag, rs)
            t_F = flip(s, z, nz, [("act", zF, None, None, [])])[0]
            yield
            yield from small_attn(s, zF, t_F, w_s("qkv"), None, None, None, "causal", t_ws, N)
            b, ps, m = N["o"]
            a = cp("act", oF, ps, m)
            s.read(b, a)
            b, ps, fr = s.one()
            for t in range(4):
                m = mm(ps[:, 128 * t:128 * t + 128], oF[:, 128 * t:128 * t + 128], w_s("lo"), True, True, fr, a)
            r = tt("pool", z, xi, bc(rw("bout"), 1, 4), ALU.add, t_F)
            yield
            a = tt("dve", xi, v3(ps, 4), z, ALU.add, m, r)
            s.read(b, a)
            xw[G] = [a]
            s.end = [a]
            yield

        def xattn1(s, G):
            s.reset()
            U = moe_bufs(s)
            sm = U["small"]
            end = s.end
            cx, it = v3(s.buf(256), 4), s.buf(256)
            iti = v3(it.bitcast(I32), 4)
            pr = v3(s.buf(256), 4)
            xi = Xv[:, 4 * G:4 * G + 4, :]

            t_c = dma(cx, wkeys[0][512 * G:512 * (G + 1), :].rearrange("(t p) k -> p t k", p=128), end)
            t_i = dma(iti, itok[512 * G:512 * (G + 1), :].rearrange("(t p) k -> p t k", p=128), end)
            ag, rs = stats(xi, 4, sm.st, sm.mv, sm.rs, xw[G], end)
            yield
            nz = norm(U["z"], xi, 4, sm.mv, sm.rs, ag, rs)
            t_F = flip(s, U["z"], nz, [("act", U["xF"], None, None, [])])[0]
            yield
            gd, prf = [], []
            for e in range(8):
                a = stt(pr, iti, float(e), cx, ALU.is_equal, ALU.mult, t_c, t_i, prf)
                a = red(U["gt"][:, :, e], pr, ALU.add, a)
                prf = [a]
                gd.append(a)
            yield
            fin = yield from experts(s, U["xF"], t_F, U["gt"], gd, (WX[:, 0:2048], WX[:, 2048:4096]), t_wx,
                                     None, None, xi, xw[G], [h[:, 0:1024] for h in U["h"]], U["gT"], 2, end)
            xw[G] = fin
            s.end = fin
            yield

        def ffn1(s, G):
            s.reset()
            U = moe_bufs(s)
            sm = U["small"]
            end = s.end
            xi = Xv[:, 4 * G:4 * G + 4, :]
            ag, rs = stats(xi, 4, sm.st, sm.mv, sm.rs, xw[G], end)
            yield
            nz = norm(U["z"], xi, 4, sm.mv, sm.rs, ag, rs)
            t_F = flip(s, U["z"], nz, [("act", U["xF"], None, None, [])])[0]
            yield
            b, ps, fr = s.one()
            for t in range(4):
                m = mm(ps[:, 8 * t:8 * t + 8], U["xF"][:, 128 * t:128 * t + 128], w_s("wg"), True, True, fr, t_F)
            l = cp("dve", U["lg"], v3(ps[:, 0:32], 4), m)
            s.read(b, l)
            gd = gates(s, U["lg"], U["gt"], [l], U["cmp"], U["aux"], 4)
            yield
            o, n = COL["g_b1"]
            o2, n2 = COL["g_b2"]
            fin = yield from experts(s, U["xF"], t_F, U["gt"], gd, (R0[:, 0:4096], R0[:, 4096:8192]), t_wl,
                                     Cl[:, o:o + n], Cl[:, o2:o2 + n2], xi, xw[G], U["h"], U["gT"], 4, end)
            st = dma(out[512 * G:512 * (G + 1), :].rearrange("(t p) d -> p t d", p=128), xi, fin)
            stores.append(st)
            xw[G] = fin
            s.end = fin
            yield

        wkeys = [ctxk_holder[0]]
        stores = []

        def phase3(s, G):
            yield from ffn0(s, G)
            yield from attn1(s, G)
            yield from xattn1(s, G)
            yield from ffn1(s, G)

        sweep(phase3, s_size, s_base)

        sems = {n: es.enter_context(nc.semaphore("s_" + n)) for n in names + dma_names}
        Q.number()
        block = es.enter_context(nc.Block())

        @block.tensor
        def _(e):
            Q.emit("pe", e, sems)

        @block.vector
        def _(e):
            Q.emit("dve", e, sems)

        @block.scalar
        def _(e):
            Q.emit("act", e, sems)

        @block.gpsimd
        def _(e):
            Q.emit("pool", e, sems)

        @block.sync
        def _(e):
            Q.emit("sp", e, sems)
            for st in stores:
                e.wait_ge(sems[st.sem], 16)


ctxk_holder = [None]


def constants():
    p = np.arange(128)
    r, q = p[:, None], p[None, :]
    same = (r // 64) == (q // 64)
    parts = {"ident": r == q, "le": same & (r <= q), "sl": same & (q < r)}
    for lv in range(4):
        n = 2 ** lv
        parts[f"nm{lv}"] = -1.0 * (((r // (2 * n)) == (q // (2 * n))) & ((q // n) % 2 == 1) & ((r // n) % 2 == 0))
    parts["nn"] = -1.0 * (same & (r // 16 < q // 16))
    t = np.arange(64)[None, :]
    parts["later"] = t > (r % 64)
    parts["causal"] = NEG * (t > (r % 64))
    parts["m32"] = (r // 32) == np.arange(4)[None, :]
    parts["m8"] = (r // 8) == np.arange(16)[None, :]
    parts["m24"] = (r // 24) == np.arange(4)[None, :]
    e = np.arange(8)
    parts["tri"] = np.broadcast_to((e[None, :] < e[:, None]).reshape(1, 64), (128, 64))
    parts["half"] = np.full((128, 1), -0.5)
    parts["one"] = np.full((128, 1), 1.0)
    parts["eids"] = np.broadcast_to(e[None, :], (128, 8))
    return np.concatenate([np.asarray(parts[n], np.float32).reshape(128, -1) for n in CST], axis=1)


def kernel(**inputs):
    import numpy as _np
    import concourse.bacc as _bacc
    from concourse import mybir as _mybir
    from concourse.bass_utils import run_bass_kernel_spmd as _run

    I = {k: _np.asarray(v) for k, v in inputs.items() if hasattr(v, "shape")}

    def rows(a, n=128):
        a = a.reshape(a.shape[0], -1)
        if a.shape[0] == n:
            return a
        return _np.concatenate([a, _np.zeros((n - a.shape[0], a.shape[1]), a.dtype)], axis=0)

    def split(a, n):
        return a.reshape(n, 128, -1).transpose(1, 0, 2).reshape(128, -1)

    A, Xn, Fn = "L0_attn_", "L0_xattn_", "L0_ffn_"
    wa = {"win": I[A + "W_in"],
          "wtm": _np.concatenate([I[A + n] for n in ("W_v", "W_g", "W_gk", "W_b", "W_q", "W_k")], axis=1),
          "wso": _np.concatenate([I[A + "W_so"][:128], rows(I[A + "W_so"][128:])], axis=1),
          "wout": split(I[A + "W_out"], 2)}
    col = {"cxw": I[A + "conv_x_w"][:, 0, :], "cxb": I[A + "conv_x_b"][:, None],
           "czw": I[A + "conv_z_w"][:, 0, :], "czb": I[A + "conv_z_b"][:, None]}
    for pf in ("a1", "a2"):
        k = Xn + pf + "_"
        for n in ("wq", "wk", "wv"):
            wa[pf + "_" + n] = rows(I[k + n].transpose(1, 0, 2).reshape(I[k + n].shape[1], 512))
        wa[pf + "_li1"] = split(I[k + "li1_w"], 4)
        wa[pf + "_li2"] = I[k + "li2_w"]
        wa[pf + "_li3"] = split(I[k + "li3_w"], 4)
        for n, m in (("xg", "lnx_g"), ("xb", "lnx_b"), ("yg", "lny_g"), ("yb", "lny_b"), ("3g", "ln3_g"), ("3b", "ln3_b")):
            col[pf + "_" + n] = rows(I[k + m][:, None])
        col[pf + "_li2b"] = I[k + "li2_b"].reshape(4, 128).T
    col["ipb"] = I[Fn + "in_proj_b"][:256].reshape(2, 128).T
    col["f_b1"] = I[Fn + "b1"].reshape(32, 128).T
    col["g_b1"] = I["L1_ffn_b1"].reshape(32, 128).T
    col["f_b2"] = rows(I[Fn + "b2"])
    col["g_b2"] = rows(I["L1_ffn_b2"])
    row = {"ln1g": Xn + "ln1_g", "ln1b": Xn + "ln1_b", "a1_li1b": Xn + "a1_li1_b", "a1_li3b": Xn + "a1_li3_b",
           "ln2g": Xn + "ln2_g", "ln2b": Xn + "ln2_b", "a2_li1b": Xn + "a2_li1_b", "a2_li3b": Xn + "a2_li3_b",
           "outb": Fn + "out_b", "f1g": Fn + "ln1_g", "f1b": Fn + "ln1_b", "f2g": Fn + "ln2_g", "f2b": Fn + "ln2_b",
           "bout": "L1_attn_b_out", "gnw": A + "g_norm_w", "alog": A + "A_log", "gateb": Fn + "gate_b"}
    row = {k: I[v] for k, v in row.items()}
    row["vb"] = I[Fn + "in_proj_b"][256:]
    row["dtb"] = _np.concatenate([I[A + "dt_bias"], I[A + "b_b"]])
    ws = {"ip": I[Fn + "in_proj_w"].T, "fo": I[Fn + "out_w"].T, "fg": I[Fn + "gate_w"].T,
          "qkv": I["L1_attn_w_qkv"], "lo": I["L1_attn_w_out"], "wg": I["L1_ffn_Wg"]}
    w1 = I[Fn + "w1"].transpose(2, 0, 1).reshape(128, -1)
    w2 = I[Fn + "w2"].transpose(2, 0, 1).reshape(4, 128, 8, 128).transpose(1, 2, 0, 3).reshape(128, -1)
    p1 = I["L1_xattn_proj_in"].transpose(2, 0, 1).reshape(128, -1)
    p2 = I["L1_xattn_proj_out"].transpose(2, 0, 1).reshape(2, 128, 8, 128).transpose(1, 2, 0, 3).reshape(128, -1)
    v1 = I["L1_ffn_W1"].transpose(1, 0, 2).reshape(128, -1)
    v2 = I["L1_ffn_W2"].reshape(8, 4, 128, 128).transpose(2, 0, 1, 3).reshape(128, -1)

    def pack(parts, order):
        return _np.ascontiguousarray(_np.concatenate([parts[n] for n in order], axis=1))

    arrays = {
        "x": I["x"].reshape(4096, 128),
        "ctx": I["ctx_512"].reshape(4096, 64),
        "ctxk": I["ctx_512"].transpose(0, 2, 1).reshape(4096, 64),
        "itok": I["itok_BxS2xS_0_7"].transpose(0, 2, 1).reshape(4096, 64),
        "cst": constants(),
        "col": pack(col, COL),
        "row": _np.broadcast_to(_np.concatenate([row[n] for n in ROW])[None, :], (128, ROW_N)),
        "wa": pack(wa, WA), "ws": pack(ws, WS),
        "wf": _np.concatenate([w1, w2], axis=1), "wx": _np.concatenate([p1, p2], axis=1),
        "wl": _np.concatenate([v1, v2], axis=1),
    }
    nc = _bacc.Bacc("TRN2", target_bir_lowering=False, num_devices=1)
    feeds, ap = {}, {}
    for name, a in arrays.items():
        a = _np.ascontiguousarray(a)
        feeds[f"in_{name}"] = a
        ap[name] = nc.dram_tensor(f"in_{name}", a.shape, _mybir.dt.from_np(a.dtype), kind="ExternalInput").ap()
    out = nc.dram_tensor("out_0", (4096, 128), _mybir.dt.float32, kind="ExternalOutput").ap()
    ctxk_holder[0] = ap["ctxk"]
    build(nc, ap["x"], ap["ctx"], ap["itok"], ap["cst"], ap["col"], ap["row"], ap["wa"], ap["ws"], ap["wf"], ap["wx"],
          ap["wl"], out)
    r = _run(nc, [feeds], core_ids=[0])
    return r.results[0]["out_0"].reshape(64, 64, 128)
```

```python
from contextlib import ExitStack

import numpy as np

import concourse.bass as bass
from concourse import mybir

F32 = mybir.dt.float32
I32 = mybir.dt.int32
ALU = mybir.AluOpType
ACT = mybir.ActivationFunctionType
AX = mybir.AxisListType.X

EPS = 1e-5
NEG = -1e30
NT = 2
W = 128 * NT
NB = 2 * NT
NG = 32 // NT
NS = 4
NP = 8 // NS


def delay(a, b):
    return 60 if a == b else 260 if b == "pe" else 200 if a == "pe" else 140

TL = 1


class Op:

    def __init__(self, eng, fn, waits, sem, ns):
        self.eng, self.fn, self.waits, self.sem, self.ns = eng, fn, waits, sem, ns
        self.used = False
        self.n = None
        self.t = None


class Queues:

    ENG = ("pe", "act", "dve", "pool", "sp")

    def __init__(self):
        self.q = {e: [] for e in self.ENG}
        self.part = {}
        self.slot = -1

    def put(self, eng, fn, *waits, sem=None, ns=150, table=None):
        flat = []

        def add(w):
            if w is None:
                return
            if isinstance(w, Op):
                w.used = True
                flat.append(w)
            else:
                for x in w:
                    add(x)

        add(waits)
        op = Op(eng, fn, flat, sem, ns)
        op.table = table
        self.part.setdefault((eng, self.slot), []).append(op)
        return op

    def merge(self):
        clock = {e: 0.0 for e in self.ENG}
        table = None
        at = {k: 0 for k in self.part}
        ready = {}
        left = sum(len(v) for v in self.part.values())
        while left:
            best = None
            for k, ops in self.part.items():
                if at[k] == len(ops):
                    continue
                if k not in ready:
                    t = 0.0
                    for w in ops[at[k]].waits:
                        if w.t is None:
                            t = None
                            break
                        t = max(t, w.t + delay(w.eng, k[0]))
                    if t is None:
                        continue
                    ready[k] = t
                start = max(clock[k[0]], ready[k])
                if best is None or (start, ready[k]) < best[0]:
                    best = ((start, ready[k]), k)
            (start, _), k = best
            op = self.part[k][at[k]]
            at[k] += 1
            del ready[k]
            left -= 1
            if op.table is not None and op.table != table:
                table = op.table
                start += 1283
            clock[k[0]] = start + op.ns
            op.t = start + op.ns + (2000 if op.sem else 0)
            self.q[k[0]].append(op)

    def number(self):
        for e in self.ENG:
            n = 0
            for op in self.q[e]:
                if op.sem is None and op.used:
                    n += 1
                    op.n = n

    def emit(self, eng, handle, sems):
        seen = {}
        for op in self.q[eng]:
            need = {}
            for w in op.waits:
                key = w.eng if w.sem is None else w.sem
                val = w.n if w.sem is None else 16
                if need.get(key, 0) < val:
                    need[key] = val
            for key, val in need.items():
                if seen.get(key, 0) < val:
                    seen[key] = val
                    handle.wait_ge(sems[key], val)
            ins = op.fn(handle)
            if op.sem is not None:
                ins.then_inc(sems[op.sem], 16)
            elif op.used:
                ins.then_inc(sems[eng], 1)


def columns(parts):
    at, out = 0, {}
    for name, n in parts:
        out[name] = (at, n)
        at += n
    return out, at


CST, CST_N = columns([
    ("ident", 128), ("le", 128), ("sl", 128), ("nm0", 128), ("nm1", 128), ("nm2", 128), ("nm3", 128), ("nn", 128),
    ("laterT", 64), ("causal", 64), ("m32", 4), ("m8", 16), ("m24", 4), ("tri", 64), ("half", 1), ("one", 1), ("eids", 8),
])
COL, COL_N = columns([
    ("cxw", 4), ("cxb", 1), ("czw", 4), ("czb", 1),
    ("a1_xg", 1), ("a1_xb", 1), ("a1_yg", 1), ("a1_yb", 1), ("a1_3g", 1), ("a1_3b", 1), ("a1_li2b", 4),
    ("a2_xg", 1), ("a2_xb", 1), ("a2_yg", 1), ("a2_yb", 1), ("a2_3g", 1), ("a2_3b", 1), ("a2_li2b", 4),
    ("ipb", 2), ("f_b1", 32), ("g_b1", 32), ("f_b2", 128), ("g_b2", 128),
])
ROW, ROW_N = columns([
    ("ln1g", 128), ("ln1b", 128), ("a1_li1b", 128), ("a1_li3b", 128), ("ln2g", 128), ("ln2b", 128),
    ("a2_li1b", 128), ("a2_li3b", 128), ("vb", 128), ("outb", 128), ("f1g", 128), ("f1b", 128), ("f2g", 128), ("f2b", 128),
    ("bout", 128), ("gnw", 48), ("dtb", 8), ("alog", 4), ("gateb", 8),
])
WA, WA_N = columns([
    ("win", 256), ("wtm", 584), ("wso", 256), ("wout", 256),
    ("a1_wq", 512), ("a1_wk", 512), ("a1_wv", 512), ("a1_li1", 512), ("a1_li2", 512), ("a1_li3", 512),
    ("a2_wq", 512), ("a2_wk", 512), ("a2_wv", 512), ("a2_li1", 512), ("a2_li2", 512), ("a2_li3", 512),
])
WS, WS_N = columns([("ip", 384), ("fo", 128), ("fg", 8), ("qkv", 384), ("lo", 128), ("wg", 8)])
WM_N = 8192
WX_N = 4096


def build(nc, x, ctx, itok, cst, col, row, wa, ws, wf, wx, wl, out):
    Q = Queues()
    put = Q.put
    es = ExitStack()
    with es:
        def sb(name, cols, dt=F32):
            return es.enter_context(nc.sbuf_tensor(name, [128, cols], dt))

        X = sb("X", 32 * 128)
        Xv = X[:, :].rearrange("p (t d) -> p t d", t=32)
        Cs = sb("Cs", CST_N)
        Cl = sb("Cl", COL_N)
        Rw = sb("Rw", ROW_N)
        R0 = sb("R0", 8192)
        Wsm = sb("Wsm", WS_N)
        EA = sb("EA", 4)
        AR_N = 35200
        AR = sb("AR", AR_N)
        PS = es.enter_context(nc.psum_tensor("PS", [128, 8, 512], F32))

        names = list(Queues.ENG)
        dma_names = []

        def c(name, a=0, b=None):
            o, n = CST[name]
            return Cs[:, o + a:o + (n if b is None else b)]

        def cl(name, j=0):
            o, n = COL[name]
            return Cl[:, o + j:o + j + 1]

        def rw(name):
            o, n = ROW[name]
            return Rw[:, o:o + n]

        def w_a(name):
            o, n = WA[name]
            return R0[:, o:o + n]

        def w_s(name):
            o, n = WS[name]
            return Wsm[:, o:o + n]

        ID = c("ident")

        def dma(dst, src, *waits):
            name = f"d{len(dma_names)}"
            dma_names.append(name)
            return put("sp", lambda e: e.dma_start(dst, src), *waits, sem=name)

        def cost(eng, o):
            n = 1
            for d in o.shape[1:]:
                n *= d
            return {"act": 100 + 0.8 * n, "dve": 70 + 1.04 * n, "pool": 60 + 2.2 * n, "pools": 100 + 4.0 * n, "pow": 180 * n}[eng]

        def mm(o, l, r, start, stop, *w):
            return put("pe", lambda e: e.matmul(o, l, r, start=start, stop=stop), *w, ns=1.75 * max(int(np.prod(r.shape[1:])), 64))

        def tr(o, i, *w):
            n = i.shape[0]
            return put("pe", lambda e: e.transpose(o, i, ID[0:n, 0:n]), *w, ns=107)

        def act(o, i, f, *w, bias=0.0, scale=1.0):
            return put("act", lambda e: e.activation(o, i, f, bias=bias, scale=scale), *w, ns=cost("act", o) + (60 if not isinstance(scale, float) else 0),
                       table=f if f in (ACT.Exp, ACT.Silu, ACT.Gelu, ACT.Ln) else None)

        def tt(eng, o, a, b, op, *w):
            return put(eng, lambda e: e.tensor_tensor(o, a, b, op), *w, ns=cost("pow" if op == ALU.pow else eng, o))

        def ts(eng, o, a, s1, s2, op0, op1, *w):
            if op1 is None:
                return put(eng, lambda e: e.tensor_scalar(o, a, s1, None, op0), *w, ns=cost("pools" if eng == "pool" else eng, o))
            return put(eng, lambda e: e.tensor_scalar(o, a, s1, s2, op0, op1), *w, ns=cost("pools" if eng == "pool" else eng, o))

        def stt(o, a, s, b, op0, op1, *w):
            return put("dve", lambda e: e.scalar_tensor_tensor(out=o, in0=a, scalar=s, in1=b, op0=op0, op1=op1), *w, ns=cost("dve", o))

        def red(o, a, op, *w):
            return put("dve", lambda e: e.tensor_reduce(o, a, AX, op), *w, ns=cost("dve", a))

        def cp(eng, o, a, *w):
            if eng == "act":
                return act(o, a, ACT.Copy, *w)
            return put(eng, lambda e: e.tensor_copy(o, a), *w, ns=cost(eng, o))

        def bc(ap, dim, n):
            return ap.unsqueeze(dim).broadcast_to(list(ap.shape[:dim]) + [n] + list(ap.shape[dim:]))

        class Slot:

            def __init__(self, i):
                self.i = i
                self.turn = 0
                self.free = [[] for _ in range(NP)]
                self.end = []
                self.base, self.size = 0, 0
                self.at = 0

            def one(self):
                b = self.turn % NP
                self.turn += 1
                return b, PS[:, NP * self.i + b, :], self.free[b]

            def two(self):
                if self.turn % 2:
                    self.turn += 1
                b = self.turn % NP
                self.turn += 2
                p = NP * self.i + b
                return b, PS[:, p:p + 2, :].rearrange("p a n -> p (a n)"), self.free[b] + self.free[b + 1]

            def read(self, b, tok, n=1):
                for j in range(n):
                    self.free[b + j] = [tok] if isinstance(tok, Op) else list(tok)

            def reset(self):
                self.at = self.base

            def buf(self, n):
                a = self.at
                self.at += n
                assert self.at <= self.base + self.size, (self.at - self.base, self.size)
                return AR[:, a:a + n]

        t_cst = dma(Cs[:, :], cst)
        t_x = []
        for g in range(NG):
            t_x.append(dma(Xv[:, NT * g:NT * g + NT, :], x[W * g:W * (g + 1), :].rearrange("(t p) d -> p t d", p=128)))
            if g == 0:
                t_col = dma(Cl[:, :], col)
                t_wa0 = dma(R0[:, 0:1352], wa[:, 0:1352])
                t_row = dma(Rw[:, :], row)
        t_wa1 = dma(R0[:, 1352:WA_N], wa[:, 1352:WA_N])
        t_ws = dma(Wsm[:, :], ws)
        t_ea = act(EA[:, :], rw("alog"), ACT.Exp, t_row)

        xw = [[t] for t in t_x]

        def stats(src, n, st, mv, rs, *w):
            last = []
            for t in range(n):
                a = put("dve", lambda e, t=t: e.bn_stats(st[:, t, :], src[:, t, :]), *w)
                last.append(a)
            ag = [put("dve", lambda e, t=t: e.bn_aggr(mv[:, t, :], st[:, t, :]), last[t]) for t in range(n)]
            a = ts("dve", rs, mv[:, :, 1], EPS, None, ALU.add, None, ag)
            half = c("half").broadcast_to([128, n])
            b = tt("pool", rs, rs, half, ALU.pow, a, t_cst)
            return ag[-1], b

        def norm(dst, src, n, mv, rs, *w, eng="dve"):
            return [ts(eng, dst[:, t, :], src[:, t, :], mv[:, t, 0:1], rs[:, t:t + 1], ALU.subtract, ALU.mult, *w)
                    for t in range(n)]

        def v3(ap, a):
            return ap.rearrange("p (a b) -> p a b", a=a)

        def flip(s, src, waits, outs):
            b, ps, fr = s.one()
            n = src.shape[2]
            ps = ps[:, 0:W]
            for t in range(NT):
                last = tr(ps[0:n, 128 * t:128 * t + 128], src[:, t, :], fr, waits[t] if len(waits) == NT else waits, t_cst)
            done = []
            for eng, o, sc, bi, w in outs:
                if sc is None:
                    done.append(cp(eng, o, ps[0:n, :], last, w))
                elif eng == "act":
                    done.append(act(o, ps[0:n, :], ACT.Identity, last, w, t_col, done[-1:], bias=bi, scale=sc))
                else:
                    done.append(ts(eng, o, ps[0:n, :], sc, bi, ALU.mult, ALU.add, last, w, t_col, done[-1:]))
            s.read(b, done)
            return done

        class Small:
            def __init__(self, s):
                self.st = v3(s.buf(6 * NT), NT)
                self.mv = v3(s.buf(2 * NT), NT)
                self.rs = s.buf(NT)

        def quads(s, D, project, tail, qm, kF, V, v_done, B, oT, scale, mode):
            NA = 2 * NB
            qv = qm.rearrange("p (b j s) -> p b j s", b=NB, j=4)
            P, mx, sm, PT = B["P"], B["mx"], B["sm"], B["PT"]
            P3 = P.rearrange("p (a t) -> p a t", t=64)

            def scores(tok):
                b, S, fr = s.one()
                for i in range(NB):
                    for j in range(4):
                        p, h = j // 2, 64 * (j % 2)
                        last = mm(S[h:h + 64, p * W + i * 64:p * W + i * 64 + 64], qv[:, i, j, :],
                                  kF[:, 64 * i:64 * i + 64], True, True, fr, tok)
                B["qm_free"] = [last]
                return b, S, last

            nxt = scores(project(0))
            yield
            done = []
            for g in range(4):
                b, S, last = nxt
                S3 = S.rearrange("p (a t) -> p a t", t=64)
                if mode == "causal":
                    a = tt("dve", P3, S3, bc(c("causal"), 1, NA), ALU.add, last, B["P_free"])
                    s.read(b, a)
                    m = red(mx, P3, ALU.max, a, B["mx_free"])
                    a = tt("dve", P3, P3, bc(mx, 2, 64), ALU.subtract, m)
                else:
                    m = red(mx, S3, ALU.max, last, B["mx_free"])
                    a = tt("dve", P3, S3, bc(mx, 2, 64), ALU.subtract, m, B["P_free"])
                    s.read(b, a)
                B["mx_free"] = [a]
                e = act(P, P, ACT.Exp, a, scale=scale)
                yield
                if g < 3:
                    tok = project(g + 1)
                r = red(sm, P3, ALU.add, e, B["sm_free"])
                r = put("dve", lambda e_: e_.reciprocal(sm, sm), r, ns=119)
                yield
                b, T, fr = s.one()
                for i in range(NB):
                    last = tr(T[:, 128 * i:128 * i + 128], P[:, 128 * i:128 * i + 128], fr, e)
                B["P_free"] = [last, r]
                if mode == "later":
                    t0 = tt("dve", v3(PT, NA), v3(T, NA), bc(c("laterT"), 1, NA), ALU.mult, last, B["PT_free"])
                else:
                    t0 = cp("act", PT, T, last, B["PT_free"])
                s.read(b, t0)
                yield
                b, O, fr = s.one()
                for p in range(2):
                    for i in range(NT):
                        col0 = (i * 2 + p) * 4 * D
                        last = mm(O[:, col0:col0 + 4 * D], PT[:, p * W + i * 128:p * W + i * 128 + 128],
                                  V[:, i, :, (4 * g + 2 * p) * D:(4 * g + 2 * p + 2) * D], True, True, fr, t0, v_done)
                B["PT_free"] = [last]
                if g < 3:
                    nxt = scores(tok)
                h0 = 0 if D == 32 else 4 * g
                part = []
                for be in range(2):
                    for pi in range(2):
                        i0 = O[64 * pi:64 * pi + 64, 0:8 * NT * D].rearrange(
                            "p (i a e h d) -> p i a e h d", i=NT, a=2, e=2, h=2)[:, :, :, be, pi, :]
                        o0 = oT[64 * be:64 * be + 64, :, :].rearrange(
                            "p i (h d) -> p i h d", d=D)[:, :, h0 + pi:h0 + pi + 3:2, :]
                        r0 = sm[64 * pi:64 * pi + 64, :].rearrange("p (a i e) -> p i a e", a=2, i=NT)[:, :, :, be]
                        part.append(tt("dve", o0, i0, bc(r0, 3, D), ALU.mult, last, r, B["oT_free"]))
                s.read(b, part)
                B["sm_free"] = part
                B["o_done"] = part
                done += part
                if tail is not None:
                    tail(g)
                yield
            B["o_done"] = done

        def zero_half(V, *w):
            return [put("dve", lambda h, e=e: h.memset(V[64 * e:64 * e + 64, :, 1 - e, :], 0.0), *w, ns=500) for e in range(2)]

        def attn_bufs(s):
            return {"P": s.buf(2 * W), "mx": s.buf(2 * NB), "sm": s.buf(2 * NB), "PT": s.buf(2 * W),
                    "P_free": [], "mx_free": [], "sm_free": [], "PT_free": [], "qm_free": [], "oT_free": []}

        def mha(s, pf, xin, xin_done, xb, B, U, mode, ystuff):
            sm = U["small"]
            zx, zy = U["zx"], U["zy"]
            ag, rs = stats(xin, NT, sm.st, sm.mv, sm.rs, xin_done)
            yield
            nz = norm(U["z"], xin, NT, sm.mv, sm.rs, ag, rs)
            t_xb = tt("pool", xb, xin, bc(rw(pf + "_li1b"), 1, NT), ALU.add, xin_done, t_row, U["xb_free"])
            yield
            outs = [("act", zx, cl(pf + "_xg"), cl(pf + "_xb"), U["z_free"])]
            if ystuff is None:
                outs.append(("dve", zy, cl(pf + "_yg"), cl(pf + "_yb"), U["z_free"]))
            d = flip(s, U["z"], nz, outs)
            t_zx = d[0]
            if ystuff is None:
                t_zy = d[1]
                KY = 128
            else:
                yT, t_y = ystuff
                t_zy = flip(s, yT, t_y, [("act", zy[0:64, :], cl(pf + "_yg")[0:64], cl(pf + "_yb")[0:64], U["z_free"])])[0]
                KY = 64
            yield
            V = U["V"]
            v_done = []
            for t in range(NT):
                b, ps, fr = s.one()
                m = mm(ps, zy[0:KY, 128 * t:128 * t + 128], w_a(pf + "_wv")[0:KY, :], True, True, fr, t_zy, t_wa1)
                eng = "act" if t % 2 else "dve"
                part = [cp(eng, V[64 * e:64 * e + 64, t, e, :], ps[64 * e:64 * e + 64, :], m) for e in range(2)]
                v_done += part
                s.read(b, part)
            yield
            oF_done = []
            oT = U["oT"]

            def project(g):
                b, ps, fr = s.one()
                ps = ps[:, 0:W]
                m = mm(ps, w_a(pf + "_wq")[:, 128 * g:128 * g + 128], zx, True, True, fr, t_zx, t_wa1)
                qv = U["qm"].rearrange("p (b j s) -> p b j s", b=NB, j=4)
                q_done = []
                for j in range(4):
                    i0 = ps.rearrange("p (b s) -> p b s", b=NB)
                    if g % 2:
                        q_done.append(act(qv[:, :, j, :], i0, ACT.Copy, m, B["qm_free"], scale=c("m32", j, j + 1)))
                    else:
                        q_done.append(ts("dve", qv[:, :, j, :], i0, c("m32", j, j + 1), None, ALU.mult, None, m, B["qm_free"]))
                s.read(b, q_done)
                b, ps, fr = s.one()
                ps = ps[:, 0:W]
                m = mm(ps, w_a(pf + "_wk")[0:KY, 128 * g:128 * g + 128], zy[0:KY, :], True, True, fr, t_zy)
                k_done = cp("act", U["kF"], ps, m, B["qm_free"])
                s.read(b, k_done)
                return q_done, k_done

            def tail(g):
                b, ps, fr = s.one()
                for t in range(NT):
                    m = tr(ps[:, 128 * t:128 * t + 128], oT[:, t, :], fr, B["o_done"])
                B["oT_free"] = [m]
                oF_done.append(cp("act", U["oF"][:, W * g:W * g + W], ps[:, 0:W], m))
                s.read(b, oF_done[-1])

            yield from quads(s, 32, project, tail, U["qm"], U["kF"], V, [v_done, U["vz"]], B, oT, 32 ** -0.5, mode)
            b, ps, fr = s.one()
            for t in range(NT):
                for g in range(4):
                    m = mm(ps[:, 128 * t:128 * t + 128], U["oF"][:, W * g + 128 * t:W * g + 128 * t + 128],
                           w_a(pf + "_li1")[:, 128 * g:128 * g + 128], g == 0, g == 3, fr, oF_done)
            yield
            xo = U["xo"]
            t_xo = tt("dve", xo, v3(ps[:, 0:W], NT), xb, ALU.add, m, t_xb, U["xo_free"])
            s.read(b, t_xo)
            ag, rs = stats(xo, NT, sm.st, sm.mv, sm.rs, t_xo, nz)
            yield
            nz = norm(U["z"], xo, NT, sm.mv, sm.rs, ag, rs)
            t_r = tt("pool", xb, xin, bc(rw(pf + "_li3b"), 1, NT), ALU.add, t_xo)
            t_r = tt("pool", xb, xb, xo, ALU.add, t_r)
            yield
            t_zx = flip(s, U["z"], nz, [("act", zx, cl(pf + "_3g"), cl(pf + "_3b"), [])])[0]
            yield
            h = U["oF"]
            h_done = []
            for f in range(4):
                b, ps, fr = s.one()
                ps = ps[:, 0:W]
                mh = mm(ps, w_a(pf + "_li2")[:, 128 * f:128 * f + 128], zx, True, True, fr, t_zx)
                h_done.append(act(h[:, W * f:W * f + W], ps, ACT.Gelu, mh, m, bias=cl(pf + "_li2b", f)))
                s.read(b, h_done[-1])
            yield
            b, ps, fr = s.one()
            for t in range(NT):
                for f in range(4):
                    m = mm(ps[:, 128 * t:128 * t + 128], h[:, W * f + 128 * t:W * f + 128 * t + 128],
                           w_a(pf + "_li3")[:, 128 * f:128 * f + 128], f == 0, f == 3, fr, h_done)
            yield
            U["res"] = (b, ps, m, t_r)

        def delta(s, G):
            s.reset()
            end = s.end
            sm = Small(s)
            xn = v3(s.buf(W), NT)
            xF = s.buf(W)
            pad = [v3(s.buf(NB * 68), NB) for _ in range(2)]
            cv = [s.buf(W) for _ in range(2)]
            qk = v3(s.buf(NT * 288), NT)
            vg = v3(s.buf(NT * 392), NT)
            bv = v3(s.buf(NT * 192), NT)
            kq = s.buf(2 * W)
            km = s.buf(4 * W)
            be4, g4, e8 = v3(s.buf(4 * NT), NT), v3(s.buf(4 * NT), NT), v3(s.buf(8 * NT), NT)
            rn = s.buf(8 * NT)
            AT = [s.buf(512) for _ in range(TL)]
            MT = [s.buf(512) for _ in range(TL)]
            XX = [s.buf(512) for _ in range(TL)]
            XT = [s.buf(512) for _ in range(TL)]
            PP = [s.buf(512) for _ in range(TL)]
            ET = [s.buf(512) for _ in range(TL)]
            UU = [s.buf(192) for _ in range(TL)]
            RR = [s.buf(192) for _ in range(TL)]
            o = v3(s.buf(NT * 192), NT)
            sq = o
            sq_o = v3(km[:, 0:192 * NT], NT)
            oF = kq
            yF = cv[0]
            xi = Xv[:, NT * G:NT * G + NT, :]

            ag, rs = stats(xi, NT, sm.st, sm.mv, sm.rs, xw[G], end)
            yield
            nz = norm(xn, xi, NT, sm.mv, sm.rs, ag, rs)
            z0 = []
            for i in range(2):
                z0.append(put("pool", lambda e, i=i: e.memset(pad[i][:, :, 0:1], 0.0), end))
                z0.append(put("pool", lambda e, i=i: e.memset(pad[i][:, :, 65:67], 0.0), end))
            yield
            t_xF = flip(s, xn, nz, [("act", xF, None, None, [])])[0]
            yield
            c_done = []
            for i in range(2):
                b, ps, fr = s.one()
                ps = ps[:, 0:W]
                m = mm(ps, w_a("win")[:, 128 * i:128 * i + 128], xF, True, True, fr, t_xF, t_wa0)
                ev = cp("act", pad[i][:, :, 1:65], ps.rearrange("p (b s) -> p b s", b=NB), m)
                s.read(b, ev)
                wn, bn = ("cxw", "cxb") if i == 0 else ("czw", "czb")
                o3 = v3(cv[i], NB)
                a = ts("dve", o3, pad[i][:, :, 0:64], cl(wn, 0), cl(bn), ALU.mult, ALU.add, ev, z0, t_col)
                for j in range(1, 4):
                    a = stt(o3, pad[i][:, :, j:j + 64], cl(wn, j), o3, ALU.mult, ALU.add, a)
                c_done.append(a)
                yield
            s_done = [act(cv[i], cv[i], ACT.Silu, c_done[i]) for i in range(2)]
            yield
            xs = cv[0]
            wt = w_a("wtm")
            e_vg, e_qk = [], []
            for t in range(NT):
                b, ps, fr = s.one()
                m = mm(ps[:, 0:392], xs[:, 128 * t:128 * t + 128], wt[:, 0:392], True, True, fr, s_done)
                e_vg.append(cp("dve", vg[:, t, :], ps[:, 0:392], m))
                s.read(b, e_vg[-1])
                b, ps, fr = s.one()
                m = mm(ps[:, 0:192], xs[:, 128 * t:128 * t + 128], wt[:, 392:584], True, True, fr, s_done)
                e_qk.append(cp("act", qk[:, t, 0:192], ps[:, 0:192], m))
                s.read(b, e_qk[-1])
                if t % 2:
                    yield
            t_sg = act(vg[:, :, 192:384], vg[:, :, 192:384], ACT.Silu, e_vg)
            sq2 = sq[:, :, 0:192]
            a = tt("pool", sq2, qk[:, :, 0:192], qk[:, :, 0:192], ALU.mult, e_qk)
            yield
            rn4 = v3(rn, NT)
            a = red(rn4, sq2.rearrange("p t (h d) -> p t h d", d=24), ALU.add, a)
            a = ts("dve", rn, rn, 1e-6, None, ALU.add, None, a)
            a = act(rn, rn, ACT.Ln, a)
            a = act(rn, rn, ACT.Exp, a, scale=-0.5)
            a_n = [tt("pool", qk[:, t, 0:192].rearrange("p (h d) -> p h d", d=24), qk[:, t, 0:192].rearrange("p (h d) -> p h d", d=24),
                      bc(rn4[:, t, :], 2, 24), ALU.mult, a) for t in range(NT)]
            p8 = tt("dve", e8, vg[:, :, 384:392], bc(rw("dtb"), 1, NT), ALU.add, e_vg, t_row)
            ab = stt(g4, e8[:, :, 0:4], -1.0, e8[:, :, 0:4], ALU.mult, ALU.min, p8)
            yield
            e1 = act(be4, e8[:, :, 4:8], ACT.Exp, p8, scale=-1.0)
            e2 = act(g4, g4, ACT.Exp, ab)
            e2 = act(g4, g4, ACT.Ln, e2, bias=1.0)
            yield
            a = ts("dve", be4, be4, 1.0, None, ALU.add, None, e1)
            t_be = put("dve", lambda e: e.reciprocal(be4, be4), a)
            a = stt(g4, e8[:, :, 0:4], 0.0, g4, ALU.max, ALU.add, e2)
            t_g = stt(g4, g4, -1.0, bc(EA[:, :], 1, NT), ALU.mult, ALU.mult, a, t_ea)
            t_kb = [tt("pool", qk[:, t, 192:288].rearrange("p (h d) -> p h d", d=24), qk[:, t, 96:192].rearrange("p (h d) -> p h d", d=24),
                       bc(be4[:, t, :], 2, 24), ALU.mult, a_n, t_be) for t in range(NT)]
            t_bv = [tt("pool", bv[:, t, :].rearrange("p (h d) -> p h d", d=48), vg[:, t, 0:192].rearrange("p (h d) -> p h d", d=48),
                       bc(be4[:, t, :], 2, 48), ALU.mult, e_vg, t_be) for t in range(NT)]
            yield
            kqv = kq.rearrange("p (t a s) -> p t a s", t=NT, a=2)
            kmv = km.rearrange("p (t h s) -> p t h s", t=NT, h=4)
            kq_done = []
            for slot_i, off, eng in ((0, 192, "act"), (1, 0, "dve")):
                b, ps, fr = s.one()
                for t in range(NT):
                    m = tr(ps[0:96, 128 * t:128 * t + 128], qk[:, t, off:off + 96], fr, t_kb, a_n)
                kq_done.append(cp(eng, kqv[0:96, :, slot_i, :], v3(ps[:, 0:W], NT)[0:96], m))
                s.read(b, kq_done[-1])
            b, ps, fr = s.one()
            for t in range(NT):
                m = tr(ps[0:96, 128 * t:128 * t + 128], qk[:, t, 96:192], fr, a_n)
            km_done = []
            for h in range(4):
                o_, i_, s_ = kmv[0:96, :, h, :], v3(ps[:, 0:W], NT)[0:96], c("m24", h, h + 1)[0:96]
                if G % 2:
                    km_done.append(act(o_, i_, ACT.Copy, m, scale=s_))
                else:
                    km_done.append(ts("dve", o_, i_, s_, None, ALU.mult, None, m))
            s.read(b, km_done)
            yield
            o_done = []
            ufree = []
            for half in range(NT // TL):
                tl = list(range(TL * half, TL * half + TL))
                T = {}
                for i, t in enumerate(tl):
                    GR = v3(PP[i], 4)
                    gr = tt("dve", GR, bc(c("sl"), 1, 4), bc(g4[:, t, :], 2, 128), ALU.mult, t_g, ufree)
                    b, ps, fr = s.one()
                    for h in range(4):
                        m = mm(ps[:, 128 * h:128 * h + 128], GR[:, h, :], c("le"), True, True, fr, gr)
                    T["dt", i] = m
                    ex = act(ET[i], ps, ACT.Exp, m, ufree)
                    s.read(b, ex)
                    T["et", i] = ex
                yield
                for i, t in enumerate(tl):
                    b, ps, fr = s.two()
                    for h in range(4):
                        m = mm(ps[:, 256 * h:256 * h + 256], kmv[0:96, t, h, :], kqv[0:96, t, :, :].rearrange("p a s -> p (a s)"),
                               True, True, fr, km_done, kq_done)
                    pv = ps.rearrange("p (h a s) -> p h a s", h=4, a=2)
                    a1 = tt("dve", v3(AT[i], 4), pv[:, :, 0, :], v3(ET[i], 4), ALU.mult, m, T["et", i], ufree)
                    a2 = tt("dve", v3(MT[i], 4), pv[:, :, 1, :], v3(ET[i], 4), ALU.mult, m, T["et", i], ufree)
                    s.read(b, [a1, a2], 2)
                    T["at", i], T["mt", i] = a1, a2
                    T["mm", i] = tt("pool", v3(MT[i], 4), v3(MT[i], 4), bc(c("le"), 1, 4), ALU.mult, a2)
                yield
                for i, t in enumerate(tl):
                    a = tt("dve", v3(XT[i], 4), v3(AT[i], 4), bc(c("nm0"), 1, 4), ALU.mult, T["at", i], ufree)
                    b, ps, fr = s.one()
                    for h in range(4):
                        m = tr(ps[:, 128 * h:128 * h + 128], XT[i][:, 128 * h:128 * h + 128], fr, a)
                    T["xt", i] = tt("pool", v3(XT[i], 4), v3(XT[i], 4), bc(ID, 1, 4), ALU.add, m)
                    T["x", i] = tt("dve", v3(XX[i], 4), v3(ps, 4), bc(ID, 1, 4), ALU.add, m, ufree)
                    s.read(b, T["x", i])
                yield
                for lv in range(1, 4):
                    for i, t in enumerate(tl):
                        prev = T.get(("pm", i))
                        ak = tt("pool", v3(ET[i], 4), v3(AT[i], 4), bc(c(f"nm{lv}"), 1, 4), ALU.mult, T["at", i], T["mt", i], prev)
                        b, ps, fr = s.one()
                        for h in range(4):
                            sl_ = slice(128 * h, 128 * h + 128)
                            m = mm(ps[:, sl_], ET[i][:, sl_], XX[i][:, sl_], True, True, fr, ak, T["x", i])
                        T["pm", i] = m
                        T["p", i] = cp("act", PP[i], ps, m, T["dt", i], T.get(("pr", i)))
                        s.read(b, T["p", i])
                    yield
                    for i, t in enumerate(tl):
                        b, ps, fr = s.one()
                        for h in range(4):
                            sl_ = slice(128 * h, 128 * h + 128)
                            if lv < 3:
                                m = mm(ps[:, sl_], XT[i][:, sl_], PP[i][:, sl_], True, True, fr, T["p", i], T["xt", i])
                            else:
                                m = mm(ps[:, sl_], PP[i][:, sl_], XT[i][:, sl_], True, True, fr, T["p", i], T["xt", i])
                        T["pr", i] = m
                        if lv < 3:
                            T["x", i] = tt("dve", XX[i], ps, XX[i], ALU.add, m)
                            s.read(b, T["x", i])
                            b, ps, fr = s.one()
                            for h in range(4):
                                m = tr(ps[:, 128 * h:128 * h + 128], XX[i][:, 128 * h:128 * h + 128], fr, T["x", i])
                            T["xt", i] = cp("act", XT[i], ps, m)
                            s.read(b, T["xt", i])
                        else:
                            T["xt", i] = tt("dve", XT[i], ps, XT[i], ALU.add, m)
                            s.read(b, T["xt", i])
                    yield
                for i, t in enumerate(tl):
                    T["nn", i] = tt("pool", v3(ET[i], 4), v3(AT[i], 4), bc(c("nn"), 1, 4), ALU.mult, T["pm", i])
                    T["r", i] = t_bv[t]
                for it in range(4):
                    for i, t in enumerate(tl):
                        src = bv[:, t, :] if it == 0 else RR[i]
                        b, ps, fr = s.one()
                        for h in range(4):
                            m = mm(ps[:, 48 * h:48 * h + 48], XT[i][:, 128 * h:128 * h + 128], src[:, 48 * h:48 * h + 48],
                                   True, True, fr, T["r", i], T["xt", i])
                        T["u", i] = cp("act", UU[i], ps[:, 0:192], m, ufree if it == 0 else T["um", i])
                        s.read(b, T["u", i])
                        T["rm", i] = m
                    yield
                    if it == 3:
                        break
                    for i, t in enumerate(tl):
                        b, ps, fr = s.one()
                        for h in range(4):
                            m = mm(ps[:, 48 * h:48 * h + 48], ET[i][:, 128 * h:128 * h + 128], UU[i][:, 48 * h:48 * h + 48],
                                   True, True, fr, T["u", i], T["nn", i])
                        T["um", i] = m
                        T["r", i] = tt("dve", RR[i], ps[:, 0:192], bv[:, t, :], ALU.add, m, T["rm", i])
                        s.read(b, T["r", i])
                    yield
                for i, t in enumerate(tl):
                    b, ps, fr = s.one()
                    for h in range(4):
                        m = mm(ps[:, 48 * h:48 * h + 48], MT[i][:, 128 * h:128 * h + 128], UU[i][:, 48 * h:48 * h + 48],
                               True, True, fr, T["u", i], T["mm", i])
                    o_done.append(cp("act", o[:, t, :], ps[:, 0:192], m))
                    s.read(b, o_done[-1])
                ufree = list(o_done)
                yield
            a = tt("pool", sq_o, o, o, ALU.mult, o_done, t_kb)
            a = red(v3(rn[:, 0:4 * NT], NT), sq_o.rearrange("p t (h d) -> p t h d", d=48), ALU.add, a, t_kb)
            a = ts("dve", rn[:, 0:4 * NT], rn[:, 0:4 * NT], 1.0 / 48, EPS, ALU.mult, ALU.add, a)
            a = tt("pool", rn[:, 0:4 * NT], rn[:, 0:4 * NT], c("half").broadcast_to([128, 4 * NT]), ALU.pow, a)
            yield
            o16 = o.rearrange("p t (h d) -> p (t h) d", d=48)
            a = tt("pool", o16, o16, bc(rn[:, 0:4 * NT], 2, 48), ALU.mult, a)
            a = tt("dve", o16, o16, bc(rw("gnw"), 1, 4 * NT), ALU.mult, a)
            a = tt("dve", o, o, vg[:, :, 192:384], ALU.mult, a, t_sg)
            yield
            b, ps, fr = s.one()
            for t in range(NT):
                m = tr(ps[:, 128 * t:128 * t + 128], o[:, t, 0:128], fr, a)
            f0 = cp("act", oF[:, 0:W], ps[:, 0:W], m)
            s.read(b, f0)
            b, ps, fr = s.one()
            for t in range(NT):
                m = tr(ps[0:64, 128 * t:128 * t + 128], o[:, t, 128:192], fr, a)
            f1 = cp("act", oF[0:64, W:2 * W], ps[0:64, 0:W], m)
            s.read(b, f1)
            yield
            b, ps, fr = s.one()
            ps = ps[:, 0:W]
            mm(ps, w_a("wso")[:, 0:128], oF[:, 0:W], True, False, fr, f0)
            m = mm(ps, w_a("wso")[0:64, 128:256], oF[0:64, W:2 * W], False, True, f1)
            y = cp("act", yF, ps, m, e_vg, e_qk)
            s.read(b, y)
            yield
            b, ps, fr = s.one()
            for t in range(NT):
                mm(ps[:, 128 * t:128 * t + 128], yF[:, 128 * t:128 * t + 128], w_a("wout")[:, 0:128], True, False, fr, y)
                m = mm(ps[:, 128 * t:128 * t + 128], cv[1][:, 128 * t:128 * t + 128], w_a("wout")[:, 128:256], False, True, s_done)
            a = tt("dve", xi, v3(ps[:, 0:W], NT), xi, ALU.add, m)
            s.read(b, a)
            xw[G] = [a]
            s.end = [a]
            yield

        def xattn(s, G):
            s.reset()
            end = s.end
            sm = Small(s)
            sm2 = Small(s)
            x1 = v3(s.buf(W), NT)
            x3 = v3(s.buf(W), NT)
            eT = v3(s.buf(64 * NT), NT)
            U = {"small": sm, "z": v3(s.buf(W), NT), "zx": s.buf(W), "zy": s.buf(W), "V": s.buf(1024 * NT).rearrange("p (t e n) -> p t e n", t=NT, e=2),
                 "qm": s.buf(4 * W), "kF": s.buf(W), "oT": v3(s.buf(W), NT), "oF": s.buf(4 * W),
                 "xo": v3(s.buf(W), NT), "z_free": [], "xb_free": [], "xo_free": []}
            xb = v3(s.buf(W), NT)
            B = attn_bufs(s)
            vz = zero_half(U["V"], end)
            xi = Xv[:, NT * G:NT * G + NT, :]
            t_e = dma(eT, ctx[W * G:W * (G + 1), :].rearrange("(t p) d -> p t d", p=128), end)
            ag, rs = stats(xi, NT, sm.st, sm.mv, sm.rs, xw[G], end)
            r2 = s.buf(NT)
            a = tt("pool", r2, sm.rs, sm.rs, ALU.mult, rs, end)
            a = tt("pool", r2, r2, sm.mv[:, :, 1], ALU.mult, a)
            a = ts("pool", r2, r2, EPS, None, ALU.add, None, a)
            a = tt("pool", r2, r2, c("half").broadcast_to([128, NT]), ALU.pow, a)
            a = tt("pool", sm.rs, sm.rs, r2, ALU.mult, a)
            yield
            nz = norm(x1, xi, NT, sm.mv, sm.rs, ag, a)
            a = tt("pool", x1, x1, bc(rw("ln1g"), 1, NT), ALU.mult, nz, t_row)
            a = tt("pool", x1, x1, bc(rw("ln1b"), 1, NT), ALU.add, a)
            ag2, rs2 = stats(eT, NT, sm2.st, sm2.mv, sm2.rs, t_e, end)
            ne = norm(eT, eT, NT, sm2.mv, sm2.rs, ag2, rs2)
            yield
            U["vz"] = vz
            yield from mha(s, "a1", x1, a, xb, B, U, "later", None)
            b, ps, m, t_r = U["res"]
            a = tt("dve", xb, v3(ps[:, 0:W], NT), xb, ALU.add, m, t_r)
            s.read(b, a)
            ag, rs = stats(xb, NT, sm.st, sm.mv, sm.rs, a)
            yield
            nz = norm(x3, xb, NT, sm.mv, sm.rs, ag, rs)
            a = tt("pool", x3, x3, bc(rw("ln2g"), 1, NT), ALU.mult, nz)
            a = tt("pool", x3, x3, bc(rw("ln2b"), 1, NT), ALU.add, a)
            yield
            yield from mha(s, "a2", x3, a, xb, B, U, "full", (eT, ne))
            b, ps, m, t_r = U["res"]
            a = tt("pool", xb, xb, xi, ALU.add, t_r)
            a = tt("dve", xi, v3(ps[:, 0:W], NT), xb, ALU.add, m, a)
            s.read(b, a)
            xw[G] = [a]
            s.end = [a]
            yield

        def small_attn(s, src, src_done, wqkv, qb, kb, vb, mode, waits, N):
            qF, kF, V, qm, oT, B = N["qF"], N["kF"], N["V"], N["qm"], N["oT"], N["B"]
            b, ps, fr = s.one()
            ps = ps[:, 0:W]
            m = mm(ps, wqkv[:, 0:128], src, True, True, fr, src_done, waits)
            if qb is None:
                tq = cp("act", qF, ps, m)
            else:
                tq = act(qF, ps, ACT.Identity, m, bias=qb)
            s.read(b, tq)
            b, ps, fr = s.one()
            ps = ps[:, 0:W]
            m = mm(ps, wqkv[:, 128:256], src, True, True, fr, src_done)
            if kb is None:
                tk = cp("dve", kF, ps, m)
            else:
                tk = ts("dve", kF, ps, kb, None, ALU.add, None, m)
            s.read(b, tk)
            yield
            b, ps, fr = s.one()
            for t in range(NT):
                m = mm(ps[:, 128 * t:128 * t + 128], src[:, 128 * t:128 * t + 128], wqkv[:, 256:384], True, True, fr)
            tv = []
            for e in range(2):
                r = slice(64 * e, 64 * e + 64)
                if vb is None:
                    tv.append(cp("act", V[r, :, e, :], v3(ps[r, 0:W], NT), m))
                else:
                    tv.append(tt("dve", V[r, :, e, :], v3(ps[r, 0:W], NT), bc(vb[r], 1, NT), ALU.add, m))
            s.read(b, tv)
            tv = tv + N["vz"]
            yield

            def project(g):
                qv = qm.rearrange("p (b j s) -> p b j s", b=NB, j=4)
                qd = []
                for j in range(4):
                    i0 = qF.rearrange("p (b s) -> p b s", b=NB)
                    mk = c("m8", 4 * g + j, 4 * g + j + 1)
                    if j < 3:
                        qd.append(act(qv[:, :, j, :], i0, ACT.Copy, tq, B["qm_free"], scale=mk))
                    else:
                        qd.append(ts("dve", qv[:, :, j, :], i0, mk, None, ALU.mult, None, tq, B["qm_free"]))
                return qd, tk

            yield from quads(s, 8, project, None, qm, kF, V, tv, B, oT, N["scale"], mode)
            done = B["o_done"]
            b, ps, fr = s.one()
            for t in range(NT):
                m = tr(ps[:, 128 * t:128 * t + 128], oT[:, t, :], fr, done)
            N["o"] = (b, ps, m)
            yield

        def small_bufs(s, scale):
            V = s.buf(2 * W).rearrange("p (t e n) -> p t e n", t=NT, e=2)
            return {"qF": s.buf(W), "kF": s.buf(W), "V": V, "vz": zero_half(V, s.end), "qm": s.buf(4 * W), "oT": v3(s.buf(W), NT),
                    "B": attn_bufs(s), "scale": scale}

        def gates(s, lg, gt, waits, cmp, aux, n):
            c4 = cmp.rearrange("p (t e f) -> p t e f", t=n, e=8)
            tri = c("tri").rearrange("p (e f) -> p e f", e=8)
            rk = v3(aux[:, 0:8 * n], n)
            mx, sm = aux[:, 8 * n:9 * n], aux[:, 9 * n:10 * n]
            last = []
            for t in range(n):
                lf = bc(lg[:, t, :], 1, 8)
                le_ = bc(lg[:, t, :], 2, 8)
                a = tt("dve", c4[:, t], lf, le_, ALU.is_equal, waits)
                a = tt("dve", c4[:, t], c4[:, t], tri, ALU.mult, a)
                b = tt("dve", cmp2(s)[:, t], lf, le_, ALU.is_gt, waits)
                last.append(tt("dve", c4[:, t], c4[:, t], cmp2(s)[:, t], ALU.add, a, b))
            a = red(rk, c4, ALU.add, last)
            a = ts("dve", rk, rk, 1.5, None, ALU.is_lt, None, a)
            m = red(mx, lg, ALU.max, waits)
            b = tt("dve", gt, lg, bc(mx, 2, 8), ALU.subtract, m)
            e = act(gt, gt, ACT.Exp, b)
            e = tt("dve", gt, gt, rk, ALU.mult, e, a)
            r = red(sm, gt, ALU.add, e)
            r = put("dve", lambda h: h.reciprocal(sm, sm), r)
            return tt("dve", gt, gt, bc(sm, 2, 8), ALU.mult, r)

        def cmp2(s):
            return s.cmp2

        def experts(s, tF, t_done, gt, g_done, WE, t_w, b1, b2, acc, acc_done, hb, gT, nf, end):
            nh = len(hb)
            w1 = WE[0].rearrange("p (e f) -> p e f", e=8)
            w2 = WE[1].rearrange("p (e f d) -> p e f d", e=8, f=nf)
            if b2 is not None:
                b, ps, fr = s.one()
                for t in range(NT):
                    m = tr(ps[0:8, 128 * t:128 * t + 128], gt[:, t, :], fr, g_done)
                a = cp("act", gT[0:8, :], ps[0:8, 0:W], m, end)
                s.read(b, a)
                b, ps, fr = s.one()
                for t in range(NT):
                    m = mm(ps[:, 128 * t:128 * t + 128], gT[0:8, 128 * t:128 * t + 128], b2[0:8, :], True, True, fr, a)
                acc_done = tt("dve", acc, v3(ps[:, 0:W], NT), acc, ALU.add, m, acc_done)
                s.read(b, acc_done)
                yield
            acc_t = [acc_done] * NT
            hfree = [[] for _ in range(nh)]
            pend = None

            def second(e, hd):
                h = hb[e % nh]
                b, ps, fr = s.one()
                for t in range(NT):
                    for f in range(nf):
                        m = mm(ps[:, 128 * t:128 * t + 128], h[:, W * f + 128 * t:W * f + 128 * t + 128],
                               w2[:, e, f, :], f == 0, f == nf - 1, fr, hd)
                hfree[e % nh] = [m]
                for t in range(NT):
                    acc_t[t] = stt(acc[:, t, :], ps[:, 128 * t:128 * t + 128], gt[:, t, e:e + 1], acc[:, t, :],
                                   ALU.mult, ALU.add, m, g_done, acc_t[t])
                s.read(b, list(acc_t))

            for e in range(8):
                hd = []
                for f in range(nf):
                    b, ps, fr = s.one()
                    ps = ps[:, 0:W]
                    m = mm(ps, w1[:, e, 128 * f:128 * f + 128], tF, True, True, fr, t_done, t_w)
                    o = hb[e % nh][:, W * f:W * f + W]
                    bi = b1[:, nf * e + f:nf * e + f + 1] if b1 is not None else 0.0
                    if f % 4 == 3:
                        a = ts("dve", o, ps, bi, 0.0, ALU.add, ALU.max, m, hfree[e % nh])
                    else:
                        a = act(o, ps, ACT.Relu, m, hfree[e % nh], bias=bi)
                    s.read(b, a)
                    hd.append(a)
                    if f % 2:
                        yield
                if pend is not None:
                    second(*pend)
                    yield
                pend = (e, hd)
            second(*pend)
            yield
            return list(acc_t)

        slots = [Slot(i) for i in range(NS)]

        def sweep(gen, size, base):
            for i, s in enumerate(slots):
                s.base, s.size = base + i * size, size
                Q.slot = i
                mine = list(range(i, NG, NS))
                if i % 2 and len(gen) > 1:
                    order = [(gen[0], mine[0])]
                    for a, b in zip(mine, mine[1:]):
                        order += [(gen[0], b)] + [(f, a) for f in gen[1:]]
                    order += [(f, mine[-1]) for f in gen[1:]]
                else:
                    order = [(f, G) for G in mine for f in gen]
                for f, G in order:
                    for _ in f(s, G):
                        pass
            Q.slot = -1

        def join():
            both = [t for s in slots for t in s.end]
            for s in slots:
                s.end = list(both)
            return both

        sweep([delta, xattn], AR_N // NS, 0)
        ph1 = join()

        WM = AR[:, 0:8192]
        WX = AR[:, 8192:12288]
        CF = AR[:, 12288:16384]
        SF = WX
        t_wf = dma(WM, wf, ph1)
        t_wl = dma(R0[:, :], wl, ph1)
        s_base = 16384
        s_size = (AR_N - s_base) // NS

        sf_done = []

        def turn(s, G):
            s.reset()
            sm = Small(s)
            z = v3(s.buf(W), NT)
            xi = Xv[:, NT * G:NT * G + NT, :]
            ag, rs = stats(xi, NT, sm.st, sm.mv, sm.rs, xw[G], s.end)
            yield
            nz = norm(z, xi, NT, sm.mv, sm.rs, ag, rs)
            b, ps, fr = s.one()
            for t in range(NT):
                m = tr(ps[:, 128 * t:128 * t + 128], z[:, t, :], fr, nz[t])
            yield
            o = SF.rearrange("p (j i) -> p i j", i=64)[:, NB * G:NB * G + NB, :]
            a = cp("act" if G % 2 else "dve", o, ps[:, 0:W].rearrange("p (i j) -> p i j", i=NB), m)
            s.read(b, a)
            sf_done.append(a)
            s.end = [a]
            yield

        sweep([turn], s_size, s_base)
        join()
        cf_done = []

        def across(s, G):
            s.reset()
            N = small_bufs(s, 8 ** -0.5)
            src = SF[:, W * G:W * G + W]
            wait = [sf_done, s.end, t_ws]
            yield from small_attn(s, src, sf_done, w_s("ip"), cl("ipb", 0), cl("ipb", 1), rw("vb"), "full", wait, N)
            b, ps, m = N["o"]
            o = CF.rearrange("p (i j) -> p j i", j=64)[:, NB * G:NB * G + NB, :]
            a = cp("act", o, ps[:, 0:W].rearrange("p (j i) -> p j i", j=NB), m)
            s.read(b, a)
            cf_done.append(a)
            s.end = [a]
            yield

        sweep([across], s_size, s_base)
        ph2 = join()
        t_wx = dma(WX, wx, ph2)

        def moe_bufs(s):
            s.cmp2 = s.buf(64 * NT).rearrange("p (t e f) -> p t e f", t=NT, e=8)
            return {"small": Small(s), "z": v3(s.buf(W), NT), "x": v3(s.buf(W), NT), "xF": s.buf(W),
                    "cmp": s.buf(64 * NT), "aux": s.buf(10 * NT), "lg": v3(s.buf(8 * NT), NT), "gt": v3(s.buf(8 * NT), NT),
                    "h": [s.buf(4 * W) for _ in range(2)], "gT": s.buf(W)}

        def ffn0(s, G):
            s.reset()
            U = moe_bufs(s)
            sm = U["small"]
            xi = Xv[:, NT * G:NT * G + NT, :]
            end = s.end
            ag, rs = stats(xi, NT, sm.st, sm.mv, sm.rs, xw[G], end)
            b, ps, fr = s.one()
            for t in range(NT):
                m = mm(ps[:, 128 * t:128 * t + 128], CF[:, W * G + 128 * t:W * G + 128 * t + 128], w_s("fo"), True, True, fr, cf_done, t_ws)
            yield
            z, x1 = U["z"], U["x"]
            nz = norm(z, xi, NT, sm.mv, sm.rs, ag, rs)
            a = tt("pool", z, z, bc(rw("outb"), 1, NT), ALU.add, nz)
            a = tt("dve", z, v3(ps[:, 0:W], NT), z, ALU.add, m, a)
            s.read(b, a)
            ag, rs = stats(z, NT, sm.st, sm.mv, sm.rs, a)
            yield
            nz = norm(x1, z, NT, sm.mv, sm.rs, ag, rs)
            a = tt("pool", x1, x1, bc(rw("f1g"), 1, NT), ALU.mult, nz)
            a = tt("pool", x1, x1, bc(rw("f1b"), 1, NT), ALU.add, a)
            yield
            t_F = flip(s, x1, [a], [("act", U["xF"], None, None, [])])[0]
            yield
            b, ps, fr = s.one()
            for t in range(NT):
                m = mm(ps[:, 8 * t:8 * t + 8], U["xF"][:, 128 * t:128 * t + 128], w_s("fg"), True, True, fr, t_F)
            l = tt("dve", U["lg"], v3(ps[:, 0:8 * NT], NT), bc(rw("gateb"), 1, NT), ALU.add, m)
            s.read(b, l)
            gd = gates(s, U["lg"], U["gt"], [l], U["cmp"], U["aux"], NT)
            yield
            o, n = COL["f_b1"]
            o2, n2 = COL["f_b2"]
            fin = yield from experts(s, U["xF"], t_F, U["gt"], gd, (WM[:, 0:4096], WM[:, 4096:8192]), t_wf,
                                     Cl[:, o:o + n], Cl[:, o2:o2 + n2], x1, a, U["h"], U["gT"], 4, end)
            ag, rs = stats(x1, NT, sm.st, sm.mv, sm.rs, fin)
            yield
            nz = norm(x1, x1, NT, sm.mv, sm.rs, ag, rs)
            a = tt("pool", x1, x1, bc(rw("f2g"), 1, NT), ALU.mult, nz)
            a = tt("pool", x1, x1, bc(rw("f2b"), 1, NT), ALU.add, a)
            a = tt("dve", xi, xi, x1, ALU.add, a)
            xw[G] = [a]
            s.end = [a]
            yield

        def attn1(s, G):
            s.reset()
            sm = Small(s)
            z, zF, oF = v3(s.buf(W), NT), s.buf(W), s.buf(W)
            N = small_bufs(s, 128 ** -0.5)
            xi = Xv[:, NT * G:NT * G + NT, :]
            ag, rs = stats(xi, NT, sm.st, sm.mv, sm.rs, xw[G], s.end)
            yield
            nz = norm(z, xi, NT, sm.mv, sm.rs, ag, rs)
            t_F = flip(s, z, nz, [("act", zF, None, None, [])])[0]
            yield
            yield from small_attn(s, zF, t_F, w_s("qkv"), None, None, None, "causal", t_ws, N)
            b, ps, m = N["o"]
            a = cp("act", oF, ps[:, 0:W], m)
            s.read(b, a)
            b, ps, fr = s.one()
            for t in range(NT):
                m = mm(ps[:, 128 * t:128 * t + 128], oF[:, 128 * t:128 * t + 128], w_s("lo"), True, True, fr, a)
            r = tt("pool", z, xi, bc(rw("bout"), 1, NT), ALU.add, t_F)
            yield
            a = tt("dve", xi, v3(ps[:, 0:W], NT), z, ALU.add, m, r)
            s.read(b, a)
            xw[G] = [a]
            s.end = [a]
            yield

        def xattn1(s, G):
            s.reset()
            U = moe_bufs(s)
            sm = U["small"]
            end = s.end
            cx, it = v3(s.buf(64 * NT), NT), s.buf(64 * NT)
            iti = v3(it.bitcast(I32), NT)
            pr = v3(s.buf(64 * NT), NT)
            xi = Xv[:, NT * G:NT * G + NT, :]

            t_c = dma(cx, wkeys[0][W * G:W * (G + 1), :].rearrange("(t p) k -> p t k", p=128), end)
            t_i = dma(iti, itok[W * G:W * (G + 1), :].rearrange("(t p) k -> p t k", p=128), end)
            ag, rs = stats(xi, NT, sm.st, sm.mv, sm.rs, xw[G], end)
            yield
            nz = norm(U["z"], xi, NT, sm.mv, sm.rs, ag, rs)
            t_F = flip(s, U["z"], nz, [("act", U["xF"], None, None, [])])[0]
            yield
            gd, prf = [], []
            for e in range(8):
                a = stt(pr, iti, float(e), cx, ALU.is_equal, ALU.mult, t_c, t_i, prf)
                a = red(U["gt"][:, :, e], pr, ALU.add, a)
                prf = [a]
                gd.append(a)
            yield
            fin = yield from experts(s, U["xF"], t_F, U["gt"], gd, (WX[:, 0:2048], WX[:, 2048:4096]), t_wx,
                                     None, None, xi, xw[G], [h[:, 0:2 * W] for h in U["h"]], U["gT"], 2, end)
            xw[G] = fin
            s.end = fin
            yield

        def ffn1(s, G):
            s.reset()
            U = moe_bufs(s)
            sm = U["small"]
            end = s.end
            xi = Xv[:, NT * G:NT * G + NT, :]
            ag, rs = stats(xi, NT, sm.st, sm.mv, sm.rs, xw[G], end)
            yield
            nz = norm(U["z"], xi, NT, sm.mv, sm.rs, ag, rs)
            t_F = flip(s, U["z"], nz, [("act", U["xF"], None, None, [])])[0]
            yield
            b, ps, fr = s.one()
            for t in range(NT):
                m = mm(ps[:, 8 * t:8 * t + 8], U["xF"][:, 128 * t:128 * t + 128], w_s("wg"), True, True, fr, t_F)
            l = cp("dve", U["lg"], v3(ps[:, 0:8 * NT], NT), m)
            s.read(b, l)
            gd = gates(s, U["lg"], U["gt"], [l], U["cmp"], U["aux"], NT)
            yield
            o, n = COL["g_b1"]
            o2, n2 = COL["g_b2"]
            fin = yield from experts(s, U["xF"], t_F, U["gt"], gd, (R0[:, 0:4096], R0[:, 4096:8192]), t_wl,
                                     Cl[:, o:o + n], Cl[:, o2:o2 + n2], xi, xw[G], U["h"], U["gT"], 4, end)
            st = dma(out[W * G:W * (G + 1), :].rearrange("(t p) d -> p t d", p=128), xi, fin)
            stores.append(st)
            xw[G] = fin
            s.end = fin
            yield

        wkeys = [ctxk_holder[0]]
        stores = []

        sweep([ffn0, attn1, xattn1, ffn1], s_size, s_base)

        sems = {n: es.enter_context(nc.semaphore("s_" + n)) for n in names + dma_names}
        Q.merge()
        Q.number()
        block = es.enter_context(nc.Block())

        @block.tensor
        def _(e):
            Q.emit("pe", e, sems)

        @block.vector
        def _(e):
            Q.emit("dve", e, sems)

        @block.scalar
        def _(e):
            Q.emit("act", e, sems)

        @block.gpsimd
        def _(e):
            Q.emit("pool", e, sems)

        @block.sync
        def _(e):
            Q.emit("sp", e, sems)
            for st in stores:
                e.wait_ge(sems[st.sem], 16)


ctxk_holder = [None]


def constants():
    p = np.arange(128)
    r, q = p[:, None], p[None, :]
    same = (r // 64) == (q // 64)
    parts = {"ident": r == q, "le": same & (r <= q), "sl": same & (q < r)}
    for lv in range(4):
        n = 2 ** lv
        parts[f"nm{lv}"] = -1.0 * (((r // (2 * n)) == (q // (2 * n))) & ((q // n) % 2 == 1) & ((r // n) % 2 == 0))
    parts["nn"] = -1.0 * (same & (r // 16 < q // 16))
    t = np.arange(64)[None, :]
    parts["laterT"] = (r % 64) > t
    parts["causal"] = NEG * (t > (r % 64))
    parts["m32"] = (r // 32) == np.arange(4)[None, :]
    parts["m8"] = (r // 8) == np.arange(16)[None, :]
    parts["m24"] = (r // 24) == np.arange(4)[None, :]
    e = np.arange(8)
    parts["tri"] = np.broadcast_to((e[None, :] < e[:, None]).reshape(1, 64), (128, 64))
    parts["half"] = np.full((128, 1), -0.5)
    parts["one"] = np.full((128, 1), 1.0)
    parts["eids"] = np.broadcast_to(e[None, :], (128, 8))
    return np.concatenate([np.asarray(parts[n], np.float32).reshape(128, -1) for n in CST], axis=1)


def kernel(**inputs):
    import numpy as _np
    import concourse.bacc as _bacc
    from concourse import mybir as _mybir
    from concourse.bass_utils import run_bass_kernel_spmd as _run

    I = {k: _np.asarray(v) for k, v in inputs.items() if hasattr(v, "shape")}

    def rows(a, n=128):
        a = a.reshape(a.shape[0], -1)
        if a.shape[0] == n:
            return a
        return _np.concatenate([a, _np.zeros((n - a.shape[0], a.shape[1]), a.dtype)], axis=0)

    def split(a, n):
        return a.reshape(n, 128, -1).transpose(1, 0, 2).reshape(128, -1)

    A, Xn, Fn = "L0_attn_", "L0_xattn_", "L0_ffn_"
    wa = {"win": I[A + "W_in"],
          "wtm": _np.concatenate([I[A + n] for n in ("W_v", "W_g", "W_gk", "W_b", "W_q", "W_k")], axis=1),
          "wso": _np.concatenate([I[A + "W_so"][:128], rows(I[A + "W_so"][128:])], axis=1),
          "wout": split(I[A + "W_out"], 2)}
    col = {"cxw": I[A + "conv_x_w"][:, 0, :], "cxb": I[A + "conv_x_b"][:, None],
           "czw": I[A + "conv_z_w"][:, 0, :], "czb": I[A + "conv_z_b"][:, None]}
    for pf in ("a1", "a2"):
        k = Xn + pf + "_"
        for n in ("wq", "wk", "wv"):
            wa[pf + "_" + n] = rows(I[k + n].transpose(1, 0, 2).reshape(I[k + n].shape[1], 512))
        wa[pf + "_li1"] = split(I[k + "li1_w"], 4)
        wa[pf + "_li2"] = I[k + "li2_w"]
        wa[pf + "_li3"] = split(I[k + "li3_w"], 4)
        for n, m in (("xg", "lnx_g"), ("xb", "lnx_b"), ("yg", "lny_g"), ("yb", "lny_b"), ("3g", "ln3_g"), ("3b", "ln3_b")):
            col[pf + "_" + n] = rows(I[k + m][:, None])
        col[pf + "_li2b"] = I[k + "li2_b"].reshape(4, 128).T
    col["ipb"] = I[Fn + "in_proj_b"][:256].reshape(2, 128).T
    col["f_b1"] = I[Fn + "b1"].reshape(32, 128).T
    col["g_b1"] = I["L1_ffn_b1"].reshape(32, 128).T
    col["f_b2"] = rows(I[Fn + "b2"])
    col["g_b2"] = rows(I["L1_ffn_b2"])
    row = {"ln1g": Xn + "ln1_g", "ln1b": Xn + "ln1_b", "a1_li1b": Xn + "a1_li1_b", "a1_li3b": Xn + "a1_li3_b",
           "ln2g": Xn + "ln2_g", "ln2b": Xn + "ln2_b", "a2_li1b": Xn + "a2_li1_b", "a2_li3b": Xn + "a2_li3_b",
           "outb": Fn + "out_b", "f1g": Fn + "ln1_g", "f1b": Fn + "ln1_b", "f2g": Fn + "ln2_g", "f2b": Fn + "ln2_b",
           "bout": "L1_attn_b_out", "gnw": A + "g_norm_w", "alog": A + "A_log", "gateb": Fn + "gate_b"}
    row = {k: I[v] for k, v in row.items()}
    row["vb"] = I[Fn + "in_proj_b"][256:]
    row["dtb"] = _np.concatenate([I[A + "dt_bias"], I[A + "b_b"]])
    ws = {"ip": I[Fn + "in_proj_w"].T, "fo": I[Fn + "out_w"].T, "fg": I[Fn + "gate_w"].T,
          "qkv": I["L1_attn_w_qkv"], "lo": I["L1_attn_w_out"], "wg": I["L1_ffn_Wg"]}
    w1 = I[Fn + "w1"].transpose(2, 0, 1).reshape(128, -1)
    w2 = I[Fn + "w2"].transpose(2, 0, 1).reshape(4, 128, 8, 128).transpose(1, 2, 0, 3).reshape(128, -1)
    p1 = I["L1_xattn_proj_in"].transpose(2, 0, 1).reshape(128, -1)
    p2 = I["L1_xattn_proj_out"].transpose(2, 0, 1).reshape(2, 128, 8, 128).transpose(1, 2, 0, 3).reshape(128, -1)
    v1 = I["L1_ffn_W1"].transpose(1, 0, 2).reshape(128, -1)
    v2 = I["L1_ffn_W2"].reshape(8, 4, 128, 128).transpose(2, 0, 1, 3).reshape(128, -1)

    def pack(parts, order):
        return _np.ascontiguousarray(_np.concatenate([parts[n] for n in order], axis=1))

    arrays = {
        "x": I["x"].reshape(4096, 128),
        "ctx": I["ctx_512"].reshape(4096, 64),
        "ctxk": I["ctx_512"].transpose(0, 2, 1).reshape(4096, 64),
        "itok": I["itok_BxS2xS_0_7"].transpose(0, 2, 1).reshape(4096, 64),
        "cst": constants(),
        "col": pack(col, COL),
        "row": _np.broadcast_to(_np.concatenate([row[n] for n in ROW])[None, :], (128, ROW_N)),
        "wa": pack(wa, WA), "ws": pack(ws, WS),
        "wf": _np.concatenate([w1, w2], axis=1), "wx": _np.concatenate([p1, p2], axis=1),
        "wl": _np.concatenate([v1, v2], axis=1),
    }
    nc = _bacc.Bacc("TRN2", target_bir_lowering=False, num_devices=1)
    feeds, ap = {}, {}
    for name, a in arrays.items():
        a = _np.ascontiguousarray(a)
        feeds[f"in_{name}"] = a
        ap[name] = nc.dram_tensor(f"in_{name}", a.shape, _mybir.dt.from_np(a.dtype), kind="ExternalInput").ap()
    out = nc.dram_tensor("out_0", (4096, 128), _mybir.dt.float32, kind="ExternalOutput").ap()
    ctxk_holder[0] = ap["ctxk"]
    build(nc, ap["x"], ap["ctx"], ap["itok"], ap["cst"], ap["col"], ap["row"], ap["wa"], ap["ws"], ap["wf"], ap["wx"],
          ap["wl"], out)
    r = _run(nc, [feeds], core_ids=[0])
    return r.results[0]["out_0"].reshape(64, 64, 128)
```
